# Optimizing a Trainium2 kernel written in Bass

```python
import numpy as np
import jax
import jax.numpy as jnp

def _softmax(x, axis=-1):
    return jax.nn.softmax(x, axis=axis)

def _gelu(x):
    return jax.nn.gelu(x, approximate=True)

def _silu(x):
    return jax.nn.silu(x)

def _sigmoid(x):
    return jax.nn.sigmoid(x)

def _layernorm(x, axis=-1, eps=1e-05):
    m = jnp.mean(x, axis=axis, keepdims=True)
    v = jnp.var(x, axis=axis, keepdims=True)
    return (x - m) / jnp.sqrt(v + eps)

def _scatter_add(tgt, idx, src, axis=0):
    return tgt.at[idx].add(src)

def _segment_sum(src, seg, n):
    return jax.ops.segment_sum(src, seg, n)
kernel_name = 'mk_cond_seq_d4_seqx_r4_3467d0'

def setup_inputs(seed: int=0):
    np.random.seed(seed)
    _w = jnp.asarray

    def _rec_inputs():
        import jax
        import jax.numpy as jnp
        _rk = jax.random.key(seed)
        x = 7.22e-05 + 1 * jax.random.normal(jax.random.fold_in(_rk, 1), (16, 256, 256), jnp.float32)
        _lenS = 256 - jax.random.randint(jax.random.fold_in(_rk, 7), (16,), 0, max(1, 256 // 4) + 1, jnp.int32)
        _lenS2 = 256 - jax.random.randint(jax.random.fold_in(_rk, 8), (16,), 0, max(1, 256 // 4) + 1, jnp.int32)
        cond_256 = -0.0209273 + 1.04763 * jax.random.normal(jax.random.fold_in(_rk, 11), (16, 64), jnp.float32)
        return (x, cond_256)
    x, cond_256 = _rec_inputs()

    def _L0_cond_setup():
        import jax, jax.numpy as jnp
        import numpy as np
        from math import sqrt
        D_MODEL = 256
        N_HEADS = 16
        D_T = 64
        D_HID = 4 * D_MODEL
        EPS = 1e-06

        def _rmsnorm(x):
            return x * jax.lax.rsqrt(jnp.mean(x * x, axis=-1, keepdims=True) + EPS)

        def _ada_rmsnorm(x, t, gamma_w, beta_w):
            gamma = (t @ gamma_w.T)[:, None, :]
            beta = (t @ beta_w.T)[:, None, :]
            return gamma * _rmsnorm(x) + beta

        def _attention(x, W_q, W_k, W_v, W_o):
            b, l, dm = x.shape
            d_head = dm // N_HEADS
            scale = sqrt(N_HEADS / dm)

            def split(y):
                return y.reshape(b, l, N_HEADS, d_head).transpose(0, 2, 1, 3)
            q = split(x @ W_q.T)
            k = split(x @ W_k.T)
            v = split(x @ W_v.T)
            attn = jax.nn.softmax(scale * jnp.einsum('bnqd,bnkd->bnqk', q, k), axis=-1)
            o = jnp.einsum('bnqk,bnkd->bnqd', attn, v)
            o = o.transpose(0, 2, 1, 3).reshape(b, l, dm)
            return o @ W_o.T

        def _swiglu(x, gate_w, hidden_w, out_w, out_b):
            return jax.nn.silu(x @ gate_w.T) * (x @ hidden_w.T) @ out_w.T + out_b
        key = jax.random.key(seed)
        ks = jax.random.split(key, 16)
        s = 0.02
        inp = {'x': jax.random.normal(ks[0], (4, 512, D_MODEL), dtype=jnp.float32), 't': jax.random.normal(ks[1], (4, D_T), dtype=jnp.float32), 'attn_gamma_w': jax.random.normal(ks[2], (D_MODEL, D_T), dtype=jnp.float32) * s, 'attn_beta_w': jax.random.normal(ks[3], (D_MODEL, D_T), dtype=jnp.float32) * s, 'W_q': jax.random.normal(ks[4], (D_MODEL, D_MODEL), dtype=jnp.float32) * s, 'W_k': jax.random.normal(ks[5], (D_MODEL, D_MODEL), dtype=jnp.float32) * s, 'W_v': jax.random.normal(ks[6], (D_MODEL, D_MODEL), dtype=jnp.float32) * s, 'W_o': jax.random.normal(ks[7], (D_MODEL, D_MODEL), dtype=jnp.float32) * s, 'attn_alpha_w': jax.random.normal(ks[8], (D_MODEL, D_T), dtype=jnp.float32) * s, 'ffn_gamma_w': jax.random.normal(ks[9], (D_MODEL, D_T), dtype=jnp.float32) * s, 'ffn_beta_w': jax.random.normal(ks[10], (D_MODEL, D_T), dtype=jnp.float32) * s, 'gate_w': jax.random.normal(ks[11], (D_HID, D_MODEL), dtype=jnp.float32) * s, 'hidden_w': jax.random.normal(ks[12], (D_HID, D_MODEL), dtype=jnp.float32) * s, 'out_w': jax.random.normal(ks[13], (D_MODEL, D_HID), dtype=jnp.float32) * s, 'out_b': jnp.zeros((D_MODEL,), dtype=jnp.float32), 'ffn_alpha_w': jax.random.normal(ks[14], (D_MODEL, D_T), dtype=jnp.float32) * s}
        return inp
    _L0_cond_all = _L0_cond_setup()
    _L0_cond_in = {k: v for k, v in _L0_cond_all.items() if k in ('attn_gamma_w', 'attn_beta_w', 'W_q', 'W_k', 'W_v', 'W_o', 'attn_alpha_w', 'ffn_gamma_w', 'ffn_beta_w', 'gate_w', 'hidden_w', 'out_w', 'out_b', 'ffn_alpha_w')}
    del _L0_cond_all

    def _L1_cond_setup():
        import jax, jax.numpy as jnp
        import numpy as np
        EPS = 1e-06

        def act_quant(x):
            scale = 127.0 / jnp.clip(jnp.max(jnp.abs(x), axis=-1, keepdims=True), 1e-05, None)
            return jnp.clip(jnp.round(x * scale), -128.0, 127.0) / scale

        def weight_quant(w):
            scale = 1.0 / jnp.clip(jnp.mean(jnp.abs(w)), 1e-05, None)
            return jnp.clip(jnp.round(w * scale), -1.0, 1.0) / scale
        key = jax.random.key(seed)
        k0, k1, k2, k3, k4 = jax.random.split(key, 5)
        B, S, D, FF, C = (4, 1024, 256, 1024, 64)
        return {'x': jax.random.normal(k0, (B, S, D), jnp.float32), 'cond': jax.random.normal(k1, (B, C), jnp.float32), 'norm_w': jax.random.normal(k2, (D, C), jnp.float32) * 0.02, 'up_w': jax.random.normal(k3, (2 * FF, D), jnp.float32) * 0.02, 'down_w': jax.random.normal(k4, (D, FF), jnp.float32) * 0.02}
    _L1_cond_all = _L1_cond_setup()
    _L1_cond_in = {k: v for k, v in _L1_cond_all.items() if k in ('norm_w', 'up_w', 'down_w')}
    del _L1_cond_all

    def _L2_cond_setup():
        import jax, jax.numpy as jnp
        import numpy as np
        DIM = 256
        BN = 128
        H = 64
        DELTA_SCALE = 0.1
        key = jax.random.key(seed)
        ks = jax.random.split(key, 10)
        B, L = (16, 512)

        def init(k, shape, fan_in):
            bound = 1.0 / np.sqrt(fan_in)
            return jax.random.uniform(k, shape, jnp.float32, -bound, bound)
        return {'x': jax.random.normal(ks[0], (B, L, DIM), jnp.float32), 'h_lang': jax.random.normal(ks[1], (B, H), jnp.float32), 'Wd': init(ks[2], (BN, DIM), DIM), 'bd': init(ks[3], (BN,), DIM), 'Wu': init(ks[4], (DIM, BN), BN), 'bu': init(ks[5], (DIM,), BN), 'Wdd': init(ks[6], (BN * DIM, H), H), 'bdd': init(ks[7], (BN * DIM,), H), 'Wdu': init(ks[8], (DIM * BN, H), H), 'bdu': init(ks[9], (DIM * BN,), H)}
    _L2_cond_all = _L2_cond_setup()
    _L2_cond_in = {k: v for k, v in _L2_cond_all.items() if k in ('Wd', 'bd', 'Wu', 'bu', 'Wdd', 'bdd', 'Wdu', 'bdu')}
    del _L2_cond_all

    def _L3_cond_setup():
        import jax, jax.numpy as jnp
        import numpy as np
        EPS = 1e-05
        key = jax.random.key(seed)
        k1, k2, k3, k4 = jax.random.split(key, 4)
        b, t, d, num_con = (8, 1024, 256, 64)
        return {'input': jax.random.normal(k1, (b, t, d), dtype=jnp.float32), 'convInfo': jax.random.normal(k2, (b, num_con), dtype=jnp.float32), 'weight': jnp.ones((d,), dtype=jnp.float32), 'bias': jnp.zeros((d,), dtype=jnp.float32), 'lin_w': jax.random.normal(k3, (d, num_con), dtype=jnp.float32) * (1.0 / np.sqrt(num_con)), 'lin_b': jax.random.normal(k4, (d,), dtype=jnp.float32) * 0.01}
    _L3_cond_all = _L3_cond_setup()
    _L3_cond_in = {k: v for k, v in _L3_cond_all.items() if k in ('weight', 'bias', 'lin_w', 'lin_b')}
    del _L3_cond_all
    return {'x': x, 'cond_256': cond_256, 'L0_cond_attn_gamma_w': _L0_cond_in['attn_gamma_w'], 'L0_cond_attn_beta_w': _L0_cond_in['attn_beta_w'], 'L0_cond_W_q': _L0_cond_in['W_q'], 'L0_cond_W_k': _L0_cond_in['W_k'], 'L0_cond_W_v': _L0_cond_in['W_v'], 'L0_cond_W_o': _L0_cond_in['W_o'], 'L0_cond_attn_alpha_w': _L0_cond_in['attn_alpha_w'], 'L0_cond_ffn_gamma_w': _L0_cond_in['ffn_gamma_w'], 'L0_cond_ffn_beta_w': _L0_cond_in['ffn_beta_w'], 'L0_cond_gate_w': _L0_cond_in['gate_w'], 'L0_cond_hidden_w': _L0_cond_in['hidden_w'], 'L0_cond_out_w': _L0_cond_in['out_w'], 'L0_cond_out_b': _L0_cond_in['out_b'], 'L0_cond_ffn_alpha_w': _L0_cond_in['ffn_alpha_w'], 'L1_cond_norm_w': _L1_cond_in['norm_w'], 'L1_cond_up_w': _L1_cond_in['up_w'], 'L1_cond_down_w': _L1_cond_in['down_w'], 'L2_cond_Wd': _L2_cond_in['Wd'], 'L2_cond_bd': _L2_cond_in['bd'], 'L2_cond_Wu': _L2_cond_in['Wu'], 'L2_cond_bu': _L2_cond_in['bu'], 'L2_cond_Wdd': _L2_cond_in['Wdd'], 'L2_cond_bdd': _L2_cond_in['bdd'], 'L2_cond_Wdu': _L2_cond_in['Wdu'], 'L2_cond_bdu': _L2_cond_in['bdu'], 'L3_cond_weight': _L3_cond_in['weight'], 'L3_cond_bias': _L3_cond_in['bias'], 'L3_cond_lin_w': _L3_cond_in['lin_w'], 'L3_cond_lin_b': _L3_cond_in['lin_b']}

def reference(x, cond_256, L0_cond_attn_gamma_w, L0_cond_attn_beta_w, L0_cond_W_q, L0_cond_W_k, L0_cond_W_v, L0_cond_W_o, L0_cond_attn_alpha_w, L0_cond_ffn_gamma_w, L0_cond_ffn_beta_w, L0_cond_gate_w, L0_cond_hidden_w, L0_cond_out_w, L0_cond_out_b, L0_cond_ffn_alpha_w, L1_cond_norm_w, L1_cond_up_w, L1_cond_down_w, L2_cond_Wd, L2_cond_bd, L2_cond_Wu, L2_cond_bu, L2_cond_Wdd, L2_cond_bdd, L2_cond_Wdu, L2_cond_bdu, L3_cond_weight, L3_cond_bias, L3_cond_lin_w, L3_cond_lin_b):
    import jax
    import jax.numpy as jnp

    def _L0_cond_ref(x, t, attn_gamma_w, attn_beta_w, W_q, W_k, W_v, W_o, attn_alpha_w, ffn_gamma_w, ffn_beta_w, gate_w, hidden_w, out_w, out_b, ffn_alpha_w):
        import jax, jax.numpy as jnp
        import numpy as np
        from math import sqrt
        D_MODEL = 256
        N_HEADS = 16
        D_T = 64
        D_HID = 4 * D_MODEL
        EPS = 1e-06

        def _rmsnorm(x):
            return x * jax.lax.rsqrt(jnp.mean(x * x, axis=-1, keepdims=True) + EPS)

        def _ada_rmsnorm(x, t, gamma_w, beta_w):
            gamma = (t @ gamma_w.T)[:, None, :]
            beta = (t @ beta_w.T)[:, None, :]
            return gamma * _rmsnorm(x) + beta

        def _attention(x, W_q, W_k, W_v, W_o):
            b, l, dm = x.shape
            d_head = dm // N_HEADS
            scale = sqrt(N_HEADS / dm)

            def split(y):
                return y.reshape(b, l, N_HEADS, d_head).transpose(0, 2, 1, 3)
            q = split(x @ W_q.T)
            k = split(x @ W_k.T)
            v = split(x @ W_v.T)
            attn = jax.nn.softmax(scale * jnp.einsum('bnqd,bnkd->bnqk', q, k), axis=-1)
            o = jnp.einsum('bnqk,bnkd->bnqd', attn, v)
            o = o.transpose(0, 2, 1, 3).reshape(b, l, dm)
            return o @ W_o.T

        def _swiglu(x, gate_w, hidden_w, out_w, out_b):
            return jax.nn.silu(x @ gate_w.T) * (x @ hidden_w.T) @ out_w.T + out_b
        a_alpha = (t @ attn_alpha_w.T)[:, None, :]
        x = x + a_alpha * _attention(_ada_rmsnorm(x, t, attn_gamma_w, attn_beta_w), W_q, W_k, W_v, W_o)
        f_alpha = (t @ ffn_alpha_w.T)[:, None, :]
        return x + f_alpha * _swiglu(_ada_rmsnorm(x, t, ffn_gamma_w, ffn_beta_w), gate_w, hidden_w, out_w, out_b)

    def _L1_cond_ref(x, cond, norm_w, up_w, down_w):
        import jax, jax.numpy as jnp
        import numpy as np
        EPS = 1e-06

        def act_quant(x):
            scale = 127.0 / jnp.clip(jnp.max(jnp.abs(x), axis=-1, keepdims=True), 1e-05, None)
            return jnp.clip(jnp.round(x * scale), -128.0, 127.0) / scale

        def weight_quant(w):
            scale = 1.0 / jnp.clip(jnp.mean(jnp.abs(w)), 1e-05, None)
            return jnp.clip(jnp.round(w * scale), -1.0, 1.0) / scale
        scale = cond @ norm_w.T + 1.0
        ms = jnp.mean(x * x, axis=-1, keepdims=True)
        h = x * (scale[:, None, :] * jax.lax.rsqrt(ms + EPS))
        u = h @ up_w.T
        val, gate = jnp.split(u, 2, axis=-1)
        h = val * jax.nn.gelu(gate, approximate=False)
        hq = h + jax.lax.stop_gradient(act_quant(h) - h)
        wq = down_w + jax.lax.stop_gradient(weight_quant(down_w) - down_w)
        y = hq @ wq.T
        return y + x

    def _L2_cond_ref(x, h_lang, Wd, bd, Wu, bu, Wdd, bdd, Wdu, bdu):
        import jax, jax.numpy as jnp
        import numpy as np
        DIM = 256
        BN = 128
        H = 64
        DELTA_SCALE = 0.1
        B, L, D = x.shape
        dWd = ((h_lang @ Wdd.T + bdd) * DELTA_SCALE).reshape(B, BN, D)
        dWu = ((h_lang @ Wdu.T + bdu) * DELTA_SCALE).reshape(B, D, BN)
        Wd_b = Wd + dWd
        Wu_b = Wu + dWu
        down = jax.nn.relu(jnp.einsum('bld,bnd->bln', x, Wd_b) + bd)
        up = jnp.einsum('bln,bdn->bld', down, Wu_b) + bu
        return x + up

    def _L3_cond_ref(input, convInfo, weight, bias, lin_w, lin_b):
        import jax, jax.numpy as jnp
        import numpy as np
        EPS = 1e-05
        mean = jnp.mean(input, axis=-1, keepdims=True)
        var = jnp.mean(jnp.square(input - mean), axis=-1, keepdims=True)
        out = (input - mean) * jax.lax.rsqrt(var + EPS) * weight + bias
        tar_bias = jnp.tanh(convInfo @ lin_w.T + lin_b)[:, None, :]
        out = out + tar_bias
        return out * weight + bias
    x = _L0_cond_ref(x, cond_256, L0_cond_attn_gamma_w, L0_cond_attn_beta_w, L0_cond_W_q, L0_cond_W_k, L0_cond_W_v, L0_cond_W_o, L0_cond_attn_alpha_w, L0_cond_ffn_gamma_w, L0_cond_ffn_beta_w, L0_cond_gate_w, L0_cond_hidden_w, L0_cond_out_w, L0_cond_out_b, L0_cond_ffn_alpha_w)
    x = _L1_cond_ref(x, cond_256, L1_cond_norm_w, L1_cond_up_w, L1_cond_down_w)
    x = _L2_cond_ref(x, cond_256, L2_cond_Wd, L2_cond_bd, L2_cond_Wu, L2_cond_bu, L2_cond_Wdd, L2_cond_bdd, L2_cond_Wdu, L2_cond_bdu)
    x = _L3_cond_ref(x, cond_256, L3_cond_weight, L3_cond_bias, L3_cond_lin_w, L3_cond_lin_b)
    return x

_drawn_inputs = setup_inputs


def setup_inputs(seed=0):
    import zlib

    import numpy as np

    out = dict(_drawn_inputs(seed))
    spreads = {'L0_cond_out_b': (0.0, 2.0), 'L3_cond_weight': (1.0, 0.2), 'L3_cond_bias': (0.0, 0.1)}
    factors = {'L0_cond_attn_gamma_w': 8.0,
     'L0_cond_attn_beta_w': 8.0,
     'L0_cond_W_q': 8.0,
     'L0_cond_W_k': 8.0,
     'L0_cond_W_v': 8.0,
     'L0_cond_W_o': 8.0,
     'L0_cond_attn_alpha_w': 8.0,
     'L0_cond_ffn_gamma_w': 8.0,
     'L0_cond_ffn_beta_w': 8.0,
     'L0_cond_gate_w': 8.0,
     'L0_cond_hidden_w': 8.0,
     'L0_cond_out_w': 8.0,
     'L0_cond_ffn_alpha_w': 3.776,
     'L1_cond_norm_w': 8.0,
     'L1_cond_up_w': 2.712,
     'L1_cond_down_w': 2.716,
     'L2_cond_bd': 166.767,
     'L3_cond_lin_b': 8.0,
     'L2_cond_bu': 64.0}
    for name, (base, spread) in spreads.items():
        noise = np.random.default_rng([zlib.crc32(name.encode()), seed]).standard_normal(out[name].shape)
        drawn = base * np.exp(spread * noise) if base else spread * noise
        out[name] = jnp.asarray(drawn.astype(out[name].dtype))
    for name, factor in factors.items():
        out[name] = (out[name] * factor).astype(out[name].dtype)
    return out
```

```python
from contextlib import ExitStack

import concourse.bass as bass
from concourse import mybir

F32 = mybir.dt.float32
F32R = mybir.dt.float32r
BF16 = mybir.dt.bfloat16
ALU = mybir.AluOpType
ACT = mybir.ActivationFunctionType
AX_X = mybir.AxisListType.X

P = 128
NB, T, D = 16, 256, 256
C = 64
DC = D // P
TT = T // P
H, DH = 16, 16
NPAIR = H // 2
F = 1024
FC = F // P
UC = 4
UW = F // UC
BN = 128
SLOTS = 5
NHY, HYW = 16, 2048
MAGIC = 12582912.0
EPS_RMS, EPS_LN = 1e-6, 1e-5

A_GAMMA, A_BETA, NEG_ALPHA, F_GAMMA, F_BETA, F_ALPHA, ALPHA_B, L1_SCALE, OFFSET = range(9)
NPAR = 9


class Batch:

    def __init__(self, i, off=0):
        self.i, self.off = i, off

    def of(self, mul, add=0):
        return self.i * mul + (self.off * mul + add)

    def follows(self):
        return not isinstance(self.i, int) or self.i + self.off > 0


class Count:

    def __init__(self, sem, per=1):
        self.sem, self.per = sem, per

    def at(self, batch, k=None, back=0):
        return batch.of(self.per, (self.per if k is None else k) - back * self.per)


def known(eng, value):
    if not isinstance(value, int):
        eng.compute_val(value)
    return value


def build(nc, xT, condT, w_cond, w_qkvT, w_oT, w_ghT, w_outT, out_b, w_upT, w_downT,
          w_hyper, adapt_w, adapt_b, bd, bu, ln_w, ln_b, lin_b, ident_in, out):
    with ExitStack() as ctx:
        def sb(name, shape, dt=F32, stack=ctx):
            return stack.enter_context(nc.sbuf_tensor(name, shape, dt))

        def sem(name, per=1):
            return Count(ctx.enter_context(nc.semaphore(name)), per)

        bank = [ctx.enter_context(nc.psum_tensor(f"bank{i}", [P, 512], F32)) for i in range(8)]

        def halves(i):
            return bank[i][:].rearrange("p (a n) -> p a n", a=2)

        q_dram = nc.dram_tensor("q_dram", [H * DH, 2, T], F32, kind="Internal").ap()
        k_dram = nc.dram_tensor("k_dram", [H * DH, 2, T], F32, kind="Internal").ap()
        cond_dram = nc.dram_tensor("cond_dram", [NB, P, NPAR * DC], F32, kind="Internal").ap()
        delta_dram = nc.dram_tensor("delta_dram", [2 * NB, D * BN], F32, kind="Internal").ap()

        w_qkv = sb("w_qkv", [P, DC, 3 * D])
        w_o = sb("w_o", [P, H // 4, D])
        gh_hi = sb("gh_hi", [P, DC, 2 * F], F32R)
        gh_lo = sb("gh_lo", [P, DC, 2 * F], F32R)
        fo_hi = sb("fo_hi", [P, FC, D], F32R)
        fo_lo = sb("fo_lo", [P, FC, D], F32R)
        up_hi = sb("up_hi", [P, DC, 2 * F], F32R)
        up_lo = sb("up_lo", [P, DC, 2 * F], F32R)
        down = sb("down", [P, FC, D], BF16)
        adapt_base = sb("adapt_base", [P, 512])
        ident = sb("ident", [P, P])
        ident_bf = sb("ident_bf", [P, P], BF16)
        mean_w = sb("mean_w", [P, P])
        down_scale = sb("down_scale", [P, 1])
        bd_c = sb("bd_c", [P, 1])
        bu_c = sb("bu_c", [P, DC])
        ln_w_c = sb("ln_w_c", [P, DC])
        neg_w2 = sb("neg_w2", [P, DC])
        columns = sb("columns", [P, 3])
        eps_rms, eps_ln, idle = columns[:, 0:1], columns[:, 1:2], columns[:, 2:3]

        w_done = sem("w_done")
        zeroed, lo_done, ternary, table = sem("zeroed"), sem("lo_done"), sem("ternary"), sem("table")
        setup_act = sem("setup_act")
        setup_pe = sem("setup_pe")
        piece_in = [sem(f"piece_in{i}") for i in range(2)]
        small_in = sem("small_in")
        hyper_in = [sem(f"hyper_in{i}", 16) for i in range(4)]
        hyper_mm = sem("hyper_mm", 4)
        hyper_ev = sem("hyper_ev", 4)
        hyper_out = [sem(f"hyper_out{i}", 64) for i in range(4)]
        cond_out = sem("cond_out")

        def hyper_turns(eng, turn):
            turn(Batch(0))
            with eng.Fori(1, NHY // 4) as r:
                turn(Batch(r))

        with ExitStack() as st:
            piece = sb("piece", [P, 2, 2048], stack=st)
            hyper = sb("hyper", [P, 4, HYW], stack=st)
            hyper_s = sb("hyper_s", [P, 4, 512], stack=st)
            cond_w = sb("cond_w", [C, 8 * D], stack=st)
            cond_t = sb("cond_t", [P, 2 * NB], stack=st)
            par = sb("par", [P, NPAR, DC, NB], stack=st)
            par_t = sb("par_t", [P, NB, NPAR, DC], stack=st)
            out_b_c = sb("out_b_c", [P, DC], stack=st)
            lin_b_c = sb("lin_b_c", [P, DC], stack=st)
            ln_b_c = sb("ln_b_c", [P, DC], stack=st)
            tanh_t = sb("tanh_t", [P, DC, NB], stack=st)
            adapt_bias = sb("adapt_bias", [P, 512], stack=st)
            w_abs = sb("w_abs", [P, 1], stack=st)
            w_mean = sb("w_mean", [P, 1], stack=st)
            w_rec = sb("w_rec", [P, 1], stack=st)
            ones = sb("ones", [P, P], stack=st)

            pieces = [
                (w_ghT[0:P, :], gh_hi[:, 0, :], gh_lo[:, 0, :]),
                (w_ghT[P:D, :], gh_hi[:, 1, :], gh_lo[:, 1, :]),
                (w_outT.rearrange("(c p) n -> p c n", p=P), fo_hi[:].rearrange("p c n -> p (c n)"),
                 fo_lo[:].rearrange("p c n -> p (c n)")),
                (w_upT[0:P, :], up_hi[:, 0, :], up_lo[:, 0, :]),
                (w_upT[P:D, :], up_hi[:, 1, :], up_lo[:, 1, :]),
                (w_downT.rearrange("(c p) n -> p c n", p=P), None, None),
            ]
            NSMALL = 17
            with nc.Block() as block:

                @block.sync
                def _(sp):
                    sp.wait_ge(zeroed.sem, 2)
                    sp.dma_start(cond_t[0:C, 0:NB], condT).then_inc(small_in.sem, 16)
                    sp.dma_start(cond_t[C:P, NB:2 * NB], condT).then_inc(small_in.sem, 16)
                    sp.dma_start(cond_w[:], w_cond).then_inc(small_in.sem, 16)
                    for dst, src in ((ident, ident_in), (bd_c, bd), (adapt_base, adapt_w), (adapt_bias, adapt_b)):
                        sp.dma_start(dst[:], src).then_inc(small_in.sem, 16)
                    for dst, src in ((out_b_c, out_b), (lin_b_c, lin_b), (ln_b_c, ln_b), (ln_w_c, ln_w), (bu_c, bu)):
                        sp.dma_start(dst[:], src).then_inc(small_in.sem, 16)
                    sp.dma_start(w_qkv[:], w_qkvT.rearrange("(c p) n -> p c n", p=P)).then_inc(small_in.sem, 16)
                    wo_src = w_oT.rearrange("(t j r) n -> j r t n", j=4, r=DH)
                    for j in range(4):
                        sp.dma_start(w_o[32 * j:32 * j + DH, :, :], wo_src[j]).then_inc(small_in.sem, 16)
                    for n, (src, _, lo) in enumerate(pieces):
                        if n >= 2:
                            sp.wait_ge(lo_done.sem, n - 1)
                        dst = piece[:, n % 2, :]
                        if len(src.shape) == 3:
                            dst = dst.rearrange("p (c n) -> p c n", n=D)
                        sp.dma_start(dst, src).then_inc(piece_in[n % 2].sem, 16)
                    sp.wait_ge(table.sem, 8 + 3 * DC)
                    sp.dma_start(cond_dram.rearrange("b p k -> p b k"),
                                 par_t[:].rearrange("p b k c -> p b (k c)")).then_inc(cond_out.sem, 16)
                    sp.wait_ge(cond_out.sem, 16)

                @block.gpsimd
                def _(pool):
                    def turn(r):
                        for s in range(4):
                            if r.follows():
                                pool.wait_ge(hyper_mm.sem, hyper_mm.at(r, s + 1, back=1))
                            pool.dma_start(hyper[:, s, :], w_hyper[:, bass.ds(r.of(4 * HYW, s * HYW), HYW)])\
                                .then_inc(hyper_in[s].sem, 16)

                    hyper_turns(pool, turn)

                @block.tensor
                def _(pe):
                    pe.wait_ge(small_in.sem, 16 * NSMALL)
                    for m in range(8):
                        for c in range(DC):
                            mm = pe.matmul(bank[0][:, (m * DC + c) * NB:(m * DC + c + 1) * NB],
                                           cond_w[:, m * D + c * P:m * D + (c + 1) * P], cond_t[0:C, 0:NB],
                                           start=True, stop=True)
                    mm.then_inc(setup_pe.sem, 1)
                    pe.wait_ge(ternary.sem, 1)
                    pe.matmul(bank[1][:, 0:1], ones[:], w_abs[:], start=True, stop=True).then_inc(setup_pe.sem, 1)
                    def turn(r):
                        for s in range(4):
                            pe.wait_ge(hyper_in[s].sem, hyper_in[s].at(r))
                            if r.follows():
                                pe.wait_ge(hyper_ev.sem, hyper_ev.at(r, s + 1, back=1))
                            for j in range(4):
                                mm = pe.matmul(bank[4 + s][32 * j:32 * j + 32, :], cond_t[:],
                                               hyper[:, s, j * 512:(j + 1) * 512], start=True, stop=True,
                                               tile_position=(0, 32 * j))
                            mm.then_inc(hyper_mm.sem, 1)

                    hyper_turns(pe, turn)

                @block.scalar
                def _(act):
                    for n, (_, hi, _) in enumerate(pieces[:-1]):
                        act.wait_ge(piece_in[n % 2].sem, 16 * (n // 2 + 1))
                        act.activation(hi, piece[:, n % 2, :], ACT.Copy).then_inc(w_done.sem, 1)
                    act.wait_ge(setup_pe.sem, 1)
                    for c in range(DC):
                        act.activation(tanh_t[:, c, :], bank[0][:, (14 + c) * NB:(15 + c) * NB], ACT.Tanh,
                                       bias=lin_b_c[:, c:c + 1]).then_inc(setup_act.sem, 1)
                    def turn(r):
                        for s in range(4):
                            act.wait_ge(hyper_mm.sem, hyper_mm.at(r, s + 1))
                            if r.follows():
                                act.wait_ge(hyper_out[s].sem, hyper_out[s].at(r, back=1))
                            act.activation(hyper_s[:, s, :], bank[4 + s][:], ACT.Copy, scale=0.1)\
                                .then_inc(hyper_ev.sem, 1)
                            act.wait_ge(hyper_ev.sem, hyper_ev.at(r, s + 1))
                            for j in range(4):
                                act.dma_start(delta_dram[:, bass.ds(r.of(4 * HYW, s * HYW + j * 512), 512)],
                                              hyper_s[32 * j:32 * j + 32, s, :]).then_inc(hyper_out[s].sem, 16)

                    hyper_turns(act, turn)
                    for s in range(4):
                        act.wait_ge(hyper_out[s].sem, hyper_out[s].at(Batch(NHY // 4 - 1)))

                @block.vector
                def _(dve):
                    dve.memset(cond_t[:], 0.0).then_inc(zeroed.sem, 1)
                    dve.memset(w_o[:], 0.0).then_inc(zeroed.sem, 1)
                    dve.memset(mean_w[:], 1.0 / D)
                    dve.memset(ones[:], 1.0)
                    dve.memset(eps_rms, EPS_RMS)
                    dve.memset(eps_ln, EPS_LN)
                    for n, (_, hi, lo) in enumerate(pieces[:-1]):
                        dve.wait_ge(w_done.sem, n + 1)
                        dve.tensor_tensor(lo, piece[:, n % 2, :], hi.bitcast(F32), ALU.subtract).then_inc(lo_done.sem, 1)
                    dve.wait_ge(piece_in[1].sem, 48)
                    w = piece[:, 1, :]
                    dve.tensor_reduce(w_abs[:], w, AX_X, ALU.add, apply_absolute_value=True).then_inc(ternary.sem, 1)
                    dve.wait_ge(setup_pe.sem, 2)
                    dve.tensor_scalar(w_mean[:], bank[1][:, 0:1], 1.0 / (F * D), 1e-5, ALU.mult, ALU.max)\
                        .then_inc(ternary.sem, 1)
                    dve.wait_ge(ternary.sem, 2)
                    dve.reciprocal(w_rec[:], w_mean[:]).then_inc(ternary.sem, 1)
                    dve.wait_ge(ternary.sem, 3)
                    dve.reciprocal(down_scale[:], w_rec[:])
                    dve.tensor_scalar(w, w, w_rec[:], MAGIC, ALU.mult, ALU.add).then_inc(ternary.sem, 1)
                    dve.wait_ge(ternary.sem, 4)
                    dve.tensor_scalar(w, w, MAGIC, 1.0, ALU.subtract, ALU.min).then_inc(ternary.sem, 1)
                    dve.wait_ge(ternary.sem, 5)
                    dve.tensor_scalar(down[:].rearrange("p c n -> p (c n)"), w, -1.0, None, ALU.max)
                    dve.wait_ge(small_in.sem, 16 * NSMALL)
                    dve.tensor_copy(ident_bf[:], ident[:])
                    dve.scalar_tensor_tensor(adapt_base[:], adapt_bias[:], 0.1, adapt_base[:], ALU.mult, ALU.add)
                    src = bank[0][:, 0:16 * NB].rearrange("p (m c b) -> p m c b", m=8, c=DC)
                    dve.wait_ge(setup_act.sem, DC)
                    dve.tensor_scalar(par[:, A_GAMMA], src[:, 0], -0.5, None, ALU.mult).then_inc(table.sem, 1)
                    dve.tensor_copy(par[:, A_BETA], src[:, 1]).then_inc(table.sem, 1)
                    dve.tensor_scalar(par[:, NEG_ALPHA], src[:, 2], -1.0, None, ALU.mult).then_inc(table.sem, 1)
                    dve.tensor_scalar(par[:, F_GAMMA], src[:, 3], -0.5, None, ALU.mult).then_inc(table.sem, 1)
                    dve.tensor_copy(par[:, F_BETA], src[:, 4]).then_inc(table.sem, 1)
                    dve.tensor_scalar(par[:, L1_SCALE], src[:, 6], 1.0, -0.5, ALU.add, ALU.mult).then_inc(table.sem, 1)
                    dve.tensor_copy(par[:, F_ALPHA], src[:, 5]).then_inc(table.sem, 1)
                    for c in range(DC):
                        dve.tensor_scalar(tanh_t[:, c, :], tanh_t[:, c, :], ln_b_c[:, c:c + 1], ln_w_c[:, c:c + 1],
                                          ALU.add, ALU.mult).then_inc(table.sem, 1)
                    dve.wait_ge(table.sem, 7 + DC)
                    for c in range(DC):
                        dve.tensor_scalar(par[:, ALPHA_B, c, :], par[:, F_ALPHA, c, :], out_b_c[:, c:c + 1], None,
                                          ALU.mult).then_inc(table.sem, 1)
                        dve.tensor_scalar(par[:, OFFSET, c, :], tanh_t[:, c, :], ln_b_c[:, c:c + 1], None, ALU.add)\
                            .then_inc(table.sem, 1)
                    dve.scalar_tensor_tensor(neg_w2[:], ln_w_c[:], -0.5, ln_w_c[:], ALU.mult, ALU.mult)
                    dve.wait_ge(table.sem, 7 + 3 * DC)
                    dve.tensor_copy(par_t[:].rearrange("p b k c -> p k c b"), par[:]).then_inc(table.sem, 1)
                    dve.wait_ge(table.sem, 8 + 3 * DC)

        x_in = sb("x_in", [P, DC, T])
        x_res = sb("x_res", [P, DC, T])
        x1 = sb("x1", [P, DC, T])
        par_a1 = sb("par_a1", [P, 2, DC])
        par_a2 = sb("par_a2", [P, 3, DC])
        h1 = sb("h1", [P, DC, T])
        y1 = sb("y1", [P, T])
        k_stack = sb("k_stack", [P, H, T], F32R)
        q_stack = sb("q_stack", [P, NPAIR, T], F32R)
        few_rows = sb("few_rows", [P, T])
        max_rows = few_rows[0:H, :].bitcast(F32R)
        zero_row = few_rows[32:32 + NPAIR, :]
        one_row = few_rows[64:65, :]
        v_aug = sb("v_aug", [P, TT, H, 2 * DH])
        probs = sb("probs", [P, SLOTS, TT, T])
        qk_split = probs[:, 0:4].rearrange("p s k t -> p (s k t)").bitcast(F32R)\
            .rearrange("p (x t l n) -> p x t l n", x=2, t=2, l=2)
        neg_max = sb("neg_max", [P, TT, 2, NPAIR])
        den = sb("den", [P, 2, T])
        den_y = sb("den_y", [P, 2, T])
        o_norm = sb("o_norm", [P, 4, T])
        h2 = sb("h2", [P, DC, T])
        h2_lo = sb("h2_lo", [P, DC, T], F32R)
        y2 = sb("y2", [P, T])
        h2_hi = sb("h2_hi", [P, DC, T], F32R)
        par_f = sb("par_f", [P, 3, DC])
        silu_g = sb("silu_g", [P, 2, T])
        act_f = sb("act_f", [P, 2, T])
        act_hi = sb("act_hi", [P, 3, T], F32R)
        act_lo = sb("act_lo", [P, 3, T], F32R)
        x2_new = sb("x2_new", [P, DC, T])
        h3 = sb("h3", [P, DC, T])
        h3_lo = sb("h3_lo", [P, DC, T], F32R)
        y3 = sb("y3", [P, T])
        h3_hi = sb("h3_hi", [P, DC, T], F32R)
        x2 = sb("x2", [P, DC, T])
        gelu_g = sb("gelu_g", [P, 2, UW])
        act_u = sb("act_u", [P, TT, F])
        q_max = sb("q_max", [P, TT])
        q_clip = sb("q_clip", [P, TT])
        q_scale = sb("q_scale", [P, TT])
        q_back = sb("q_back", [P, TT])
        q_int = sb("q_int", [P, F], BF16)
        q_T = sb("q_T", [P, TT, FC, P], BF16)
        mlp_y = sb("mlp_y", [P, TT, D])
        x3 = sb("x3", [P, DC, T])
        par_g = sb("par_g", [P, DC])
        adapt = sb("adapt", [P, 512])
        adapt_h = sb("adapt_h", [P, T])
        xc = sb("xc", [P, DC, T])
        sq4 = adapt[:].rearrange("p (c t) -> p c t", c=DC)
        y4 = sb("y4", [P, T])

        x_in_dma, x_res_dma = sem("x_in_dma", 32), sem("x_res_dma", 32)
        qk_dram_w, stack_dma = sem("qk_dram_w", 32), sem("stack_dma", 16 * 14)
        max_dma = sem("max_dma", 32)
        par_f_dma, adapt_dma, out_dma = sem("par_f_dma", 16), sem("adapt_dma", 48), sem("out_dma", 16)
        n1_act, n1_pe, n1_dve = sem("n1_act", 3), sem("n1_pe"), sem("n1_dve", 6)
        n2_act, n2_pe, n2_dve, n2_hi = sem("n2_act", 3), sem("n2_pe"), sem("n2_dve", 7), sem("n2_hi")
        n3_act, n3_pe, n3_dve, n3_hi = sem("n3_act", 3), sem("n3_pe"), sem("n3_dve", 7), sem("n3_hi")
        n4_act, n4_pe, n4_dve = sem("n4_act", 2), sem("n4_pe", 2), sem("n4_dve", 7)
        q_mm, k_mm, v_mm = sem("q_mm"), sem("k_mm"), sem("v_mm")
        qk_hi, qk_lo, v_ready = sem("qk_hi", 2), sem("qk_lo", 2), sem("v_ready")
        max_mm, max_red = sem("max_mm", 16), sem("max_red", 16)
        max_t, max_row = sem("max_t"), sem("max_row")
        s_mm, s_exp, pv_mm = sem("s_mm", 16), sem("s_exp", 16), sem("pv_mm", 4)
        den_act, o_dve = sem("den_act", 4), sem("o_dve", 8)
        wo_mm, x1_dve = sem("wo_mm"), sem("x1_dve", 2)
        g_mm, g_silu, g_dve, g_hi, g_lo = (sem(n, FC) for n in ("g_mm", "g_silu", "g_dve", "g_hi", "g_lo"))
        fo_mm, x2_dve = sem("fo_mm", FC), sem("x2_dve", 4)
        u_mm, u_gelu, u_dve = sem("u_mm", 8), sem("u_gelu", 8), sem("u_dve", 8)
        q_dve, qT_mm, qT_dve = sem("q_dve", 14), sem("qT_mm", 2), sem("qT_dve", 2)
        d_mm, y_dve, yT_mm, x3_dve, x2_cp = sem("d_mm"), sem("y_dve", 2), sem("yT_mm"), sem("x3_dve"), sem("x2_cp")
        adapt_w_ready, ad_mm, ad_h, au_mm, x4_dve = (sem("adapt_w_ready"), sem("ad_mm"), sem("ad_h"), sem("au_mm"),
                                                     sem("x4_dve", 2))
        y4_ln, x5_dve = sem("y4_ln"), sem("x5_dve", 2)
        init_dve, init_dma = sem("init_dve"), sem("init_dma")

        def rows(t):
            return t.rearrange("(c p) t -> p c t", p=P)

        def bat(b):
            return b.of(1)

        def batch_of(tensor, b):
            return tensor[bass.ds(bat(b), 1)].rearrange("o a b -> (o a) b")

        def schedule(run):
            z = lambda n: Batch(0, n)
            run(z(0), None, None, z(1))
            run(z(1), z(0), None, z(2))
            run(z(2), z(1), z(0), z(3))
            return z

        def drain(run, z):
            run(z(NB - 1), z(NB - 2), z(NB - 3), None)
            run(None, z(NB - 1), z(NB - 2), None)
            run(None, None, z(NB - 1), None)

        def whole(eng, run):
            z = schedule(run)
            with eng.Fori(3, NB - 1) as i:
                run(Batch(i), Batch(i, -1), Batch(i, -2), Batch(i, 1))
            drain(run, z)

        with nc.Block() as block:

            @block.sync
            def _(sp):
                def load_x(b):
                    if b.follows():
                        sp.wait_ge(n1_dve.sem, n1_dve.at(b, back=1))
                    sp.dma_start(x_in[:], rows(batch_of(xT, b))).then_inc(x_in_dma.sem, 16)
                    sp.dma_start(par_a1[:].rearrange("p k c -> p (k c)"),
                                 batch_of(cond_dram, b)[:, A_GAMMA * DC:(A_BETA + 1) * DC]).then_inc(x_in_dma.sem, 16)

                def stack_qk(b):
                    for x, dram in enumerate((q_dram, k_dram)):
                        hi_value = known(sp, qk_hi.at(b, x + 1))
                        lo_value = known(sp, qk_lo.at(b, x + 1))
                        if b.follows():
                            left_value = known(sp, stack_dma.at(b, back=1))
                            sp.wait_ge(stack_dma.sem, left_value)
                        sp.wait_ge(qk_hi.sem, hi_value)
                        sp.wait_ge(qk_lo.sem, lo_value)
                        sp.dma_start(dram.rearrange("(t p) l n -> p t (l n)", p=P),
                                     qk_split[:, x].rearrange("p t l n -> p t (l n)").bitcast(F32)).then_inc(qk_dram_w.sem, 16)
                    if b.follows():
                        sp.wait_ge(s_mm.sem, s_mm.at(b, back=1))
                    for a in range(2):
                        sp.dma_start(q_stack[64 * a + 48:64 * a + 49, :, :].bitcast(F32), zero_row).then_inc(stack_dma.sem, 16)
                    sp.wait_ge(qk_dram_w.sem, qk_dram_w.at(b))
                    for dram, dst, parts in ((q_dram, q_stack, (0, 1, 0)), (k_dram, k_stack, (0, 0, 1))):
                        for a in range(2):
                            for c, part in enumerate(parts):
                                src = dram[:, part].rearrange("(m a r) n -> a r m n", a=2, r=DH)[a]
                                at = 64 * a + DH * c
                                to = dst[at:at + DH, :, :] if dst is q_stack else \
                                    dst[at:at + DH].rearrange("r (m a) n -> r a m n", a=2)[:, a]
                                sp.dma_start(to.bitcast(F32), src).then_inc(stack_dma.sem, 16)

                def load_res(b):
                    if b.follows():
                        res_value = known(sp, x1_dve.at(b, back=1))
                        par_value = known(sp, n2_dve.at(b, back=1))
                        sp.wait_ge(x1_dve.sem, res_value)
                        sp.wait_ge(n2_dve.sem, par_value)
                    sp.dma_start(x_res[:], rows(batch_of(xT, b))).then_inc(x_res_dma.sem, 16)
                    sp.dma_start(par_a2[:].rearrange("p k c -> p (k c)"),
                                 batch_of(cond_dram, b)[:, NEG_ALPHA * DC:(F_BETA + 1) * DC]).then_inc(x_res_dma.sem, 16)

                def run(a, f, g, nxt):
                    if a:
                        load_res(a)
                    if f:
                        if f.follows():
                            sp.wait_ge(n3_dve.sem, n3_dve.at(f, back=1))
                        sp.dma_start(par_f[:].rearrange("p k c -> p (k c)"),
                                     batch_of(cond_dram, f)[:, F_ALPHA * DC:(L1_SCALE + 1) * DC]).then_inc(par_f_dma.sem, 16)
                    if g:
                        if g.follows():
                            adapt_value = known(sp, au_mm.at(g, back=1))
                            par_value = known(sp, n4_dve.at(g, back=1))
                            sp.wait_ge(au_mm.sem, adapt_value)
                            sp.wait_ge(n4_dve.sem, par_value)
                        sp.dma_start(adapt[:, 0:256].rearrange("p (c n) -> p c n", c=DC),
                                     delta_dram[bass.ds(bat(g), 1), :].rearrange("o (c p n) -> p (o c) n", c=DC, n=BN))\
                            .then_inc(adapt_dma.sem, 16)
                        sp.dma_start(adapt[:, 256:512],
                                     delta_dram[bass.ds(g.of(1, NB), 1), :].rearrange("o (p n) -> p (o n)", n=D))\
                            .then_inc(adapt_dma.sem, 16)
                        sp.dma_start(par_g[:], batch_of(cond_dram, g)[:, OFFSET * DC:(OFFSET + 1) * DC])\
                            .then_inc(adapt_dma.sem, 16)
                    if nxt:
                        load_x(nxt)
                    if a:
                        row_value = known(sp, max_row.at(a))
                        mm_value = known(sp, max_mm.at(a))
                        sp.wait_ge(max_row.sem, row_value)
                        sp.wait_ge(max_mm.sem, mm_value)
                        for par in range(2):
                            sp.dma_start(q_stack[64 * par + 48:64 * par + 49, :, :].bitcast(F32),
                                         max_rows[NPAIR * par:NPAIR * (par + 1), :].bitcast(F32)).then_inc(max_dma.sem, 16)
                    if nxt:
                        stack_qk(nxt)
                    if g:
                        sp.wait_ge(n4_dve.sem, n4_dve.at(g))
                        sp.dma_start(rows(batch_of(out, g)), xc[:]).then_inc(out_dma.sem, 16)

                sp.wait_ge(init_dve.sem, 5)
                for h in range(H):
                    at = 64 * (h % 2) + 48
                    sp.dma_start(k_stack[at:at + 1, h, :].bitcast(F32), one_row).then_inc(init_dma.sem, 16)
                load_x(Batch(0))
                stack_qk(Batch(0))
                whole(sp, run)
                sp.wait_ge(out_dma.sem, 16 * NB)

            @block.gpsimd
            def _(pool):
                def run(a, f, g, nxt):
                    if f:
                        for c in range(FC):
                            pool.wait_ge(g_hi.sem, g_hi.at(f, c + 1))
                            if f.follows() or c > 2:
                                pool.wait_ge(fo_mm.sem, fo_mm.at(f, c - 2))
                            pool.tensor_tensor(act_lo[:, c % 3, :], act_f[:, c % 2, :], act_hi[:, c % 3, :].bitcast(F32),
                                               ALU.subtract).then_inc(g_lo.sem, 1)
                    if g:
                        pool.wait_ge(adapt_dma.sem, adapt_dma.at(g))
                        pool.tensor_tensor(adapt[:], adapt[:], adapt_base[:], ALU.add).then_inc(adapt_w_ready.sem, 1)

                whole(pool, run)

            @block.tensor
            def _(pe):
                def mean(at, src):
                    for c in range(DC):
                        mm = pe.matmul(at, mean_w[:], src[:, c, :], start=(c == 0), stop=(c == DC - 1))
                    return mm

                def norm_a(b):
                    pe.wait_ge(n1_act.sem, n1_act.at(b, 1))
                    mean(bank[5][:, 0:T], h1).then_inc(n1_pe.sem, 1)

                def project_qk(b):
                    pe.wait_ge(n1_dve.sem, n1_dve.at(b))
                    if b.follows():
                        pe.wait_ge(s_exp.sem, s_exp.at(b, back=1))
                    for x, done in ((0, q_mm), (1, k_mm)):
                        for t in range(2):
                            for c in range(DC):
                                mm = pe.matmul(halves(x)[:, t, :], w_qkv[:, c, x * D + t * P:x * D + (t + 1) * P], h1[:, c, :],
                                               start=(c == 0), stop=(c == DC - 1))
                        mm.then_inc(done.sem, 1)

                def project_v(b):
                    if b.follows():
                        pe.wait_ge(o_dve.sem, o_dve.at(b, 4, back=1))
                    for t in range(TT):
                        for c in range(DC):
                            mm = pe.matmul(halves(2)[:, t, :], h1[:, c, t * P:(t + 1) * P], w_qkv[:, c, 2 * D:3 * D],
                                           start=(c == 0), stop=(c == DC - 1))
                    mm.then_inc(v_mm.sem, 1)

                def max_scores(b, n):
                    pair, qt = n // 2, n % 2
                    if n == 0:
                        pe.wait_ge(stack_dma.sem, stack_dma.at(b))
                    if n == 0:
                        pe.wait_ge(qk_lo.sem, qk_lo.at(b, 1))
                    if n == 1:
                        pe.wait_ge(qk_lo.sem, qk_lo.at(b, 2))
                    if n == 2:
                        pe.wait_ge(v_ready.sem, v_ready.at(b))
                    if n >= 3:
                        pe.wait_ge(max_red.sem, max_red.at(b, n - 2))
                    pe.matmul(bank[n % 3][:], q_stack[:, pair, qt * P:(qt + 1) * P],
                              k_stack[:, 2 * pair:2 * pair + 2, :], start=True, stop=True).then_inc(max_mm.sem, 1)

                def max_turn(b):
                    pe.wait_ge(max_red.sem, max_red.at(b))
                    for t in range(TT):
                        mm = pe.transpose(bank[0][0:H, t * P:(t + 1) * P], neg_max[:, t].rearrange("p a m -> p (a m)"), ident[:])
                    mm.then_inc(max_t.sem, 1)

                def scores(b, h):
                    if h == 0:
                        pe.wait_ge(max_dma.sem, max_dma.at(b))
                        pe.wait_ge(max_row.sem, max_row.at(b))
                    if h >= 2:
                        pe.wait_ge(s_exp.sem, s_exp.at(b, h - 1))
                    for k in range(TT):
                        mm = pe.matmul(halves(h % 2)[:, k, :], k_stack[:, h, k * P:(k + 1) * P], q_stack[:, h // 2, :],
                                       start=True, stop=True)
                    mm.then_inc(s_mm.sem, 1)

                def attend(b, t):
                    pe.wait_ge(s_exp.sem, s_exp.at(b, 4 * t + 4))
                    pe.wait_ge(v_ready.sem, v_ready.at(b))
                    at = halves(2 + t // 2)
                    for k in range(TT):
                        for j in range(4):
                            mm = pe.matmul(at[32 * j:32 * j + 32, t % 2, :], v_aug[:, k, 4 * t + j, :], probs[:, (4 * t + j) % SLOTS, k, :],
                                           start=(k == 0), stop=(k == TT - 1), tile_position=(0, 32 * j))
                    mm.then_inc(pv_mm.sem, 1)

                def project(b):
                    pe.wait_ge(o_dve.sem, o_dve.at(b))
                    for m in range(DC):
                        for t in range(4):
                            mm = pe.matmul(halves(3)[:, m, :], w_o[:, t, m * P:(m + 1) * P], o_norm[:, t, :],
                                           start=(t == 0), stop=(t == 3))
                    mm.then_inc(wo_mm.sem, 1)

                def norm_f(b):
                    pe.wait_ge(n2_act.sem, n2_act.at(b, 1))
                    if b.follows():
                        pe.wait_ge(g_dve.sem, g_dve.at(b, back=1))
                    mean(bank[4][:, 0:T], h2[:]).then_inc(n2_pe.sem, 1)

                def gate(b, c):
                    if c == 0:
                        pe.wait_ge(n2_dve.sem, n2_dve.at(b))
                        pe.wait_ge(n2_hi.sem, n2_hi.at(b))
                    if c >= 2:
                        pe.wait_ge(g_dve.sem, g_dve.at(b, c - 1))
                    at = halves(4 + c % 2)
                    for x in range(2):
                        n = 0
                        for w, h in ((gh_hi, h2_hi), (gh_lo, h2_hi), (gh_hi, h2_lo)):
                            for d in range(DC):
                                mm = pe.matmul(at[:, x, :], w[:, d, x * F + c * P:x * F + (c + 1) * P], h[:, d, :],
                                               start=(n == 0), stop=(n == 5))
                                n += 1
                    mm.then_inc(g_mm.sem, 1)

                def ffn_out(b, c):
                    pe.wait_ge(g_lo.sem, g_lo.at(b, c + 1))
                    if c == 0:
                        pe.wait_ge(x1_dve.sem, x1_dve.at(b))
                    for m in range(DC):
                        for n, (w, h) in enumerate(((fo_hi, act_hi), (fo_lo, act_hi), (fo_hi, act_lo))):
                            mm = pe.matmul(halves(3)[:, m, :], w[:, c, m * P:(m + 1) * P], h[:, c % 3, :],
                                           start=(c == 0 and m == 0 and n == 0), stop=(c == FC - 1 and n == 2),
                                           skip_group_check=True)
                    mm.then_inc(fo_mm.sem, 1)

                def norm_g(b):
                    pe.wait_ge(n3_act.sem, n3_act.at(b, 1))
                    mean(bank[4][:, 0:T], h3[:]).then_inc(n3_pe.sem, 1)

                def up(b, n):
                    t, c = n // UC, n % UC
                    if n == 0:
                        pe.wait_ge(n3_dve.sem, n3_dve.at(b))
                        pe.wait_ge(n3_hi.sem, n3_hi.at(b))
                        if b.follows():
                            pe.wait_ge(ad_h.sem, ad_h.at(b, back=1))
                            pe.wait_ge(x4_dve.sem, x4_dve.at(b, back=1))
                            pe.wait_ge(n4_dve.sem, n4_dve.at(b, 5, back=1))
                    if n >= 2:
                        pe.wait_ge(u_dve.sem, u_dve.at(b, n - 1))
                    at = halves(6 + n % 2)
                    for x in range(2):
                        i = 0
                        for w, h in ((up_hi, h3_hi), (up_lo, h3_hi), (up_hi, h3_lo)):
                            for d in range(DC):
                                mm = pe.matmul(at[:, x, :], h[:, d, t * P:(t + 1) * P],
                                               w[:, d, x * F + c * UW:x * F + (c + 1) * UW], start=(i == 0), stop=(i == 5))
                                i += 1
                    mm.then_inc(u_mm.sem, 1)

                def q_turn(b, t):
                    pe.wait_ge(q_dve.sem, q_dve.at(b, 7 * t + 7))
                    at = bank[7 - t][:].bitcast(BF16).rearrange("p (c n) -> p c n", n=P)
                    if t == 1:
                        pe.wait_ge(u_dve.sem, u_dve.at(b))
                    for c in range(FC):
                        mm = pe.transpose(at[:, c, :], q_int[:, c * P:(c + 1) * P], ident_bf[:])
                    mm.then_inc(qT_mm.sem, 1)

                def mlp_down(b):
                    pe.wait_ge(u_dve.sem, u_dve.at(b))
                    pe.wait_ge(qT_dve.sem, qT_dve.at(b))
                    for t in range(TT):
                        for c in range(FC):
                            mm = pe.matmul(halves(7)[:, t, :], q_T[:, t, c, :], down[:, c, :], start=(c == 0), stop=(c == FC - 1))
                    mm.then_inc(d_mm.sem, 1)

                def y_turn(b):
                    pe.wait_ge(y_dve.sem, y_dve.at(b))
                    for m in range(DC):
                        for t in range(TT):
                            mm = pe.transpose(halves(6)[:, m, t * P:(t + 1) * P], mlp_y[:, t, m * P:(m + 1) * P], ident[:])
                    mm.then_inc(yT_mm.sem, 1)

                def adapter_down(b):
                    pe.wait_ge(adapt_w_ready.sem, adapt_w_ready.at(b))
                    pe.wait_ge(x3_dve.sem, x3_dve.at(b))
                    for c in range(DC):
                        mm = pe.matmul(bank[7][:, 0:T], adapt[:, c * BN:(c + 1) * BN], x3[:, c, :], start=(c == 0), stop=(c == DC - 1))
                    mm.then_inc(ad_mm.sem, 1)

                def adapter_up(b):
                    pe.wait_ge(ad_h.sem, ad_h.at(b))
                    for m in range(DC):
                        mm = pe.matmul(halves(6)[:, m, :], adapt[:, 256 + m * P:256 + (m + 1) * P], adapt_h[:], start=True, stop=True)
                    mm.then_inc(au_mm.sem, 1)

                def ln_mean(b):
                    pe.wait_ge(x4_dve.sem, x4_dve.at(b))
                    mean(bank[7][:, 0:T], x3).then_inc(n4_pe.sem, 1)

                def ln_var(b):
                    pe.wait_ge(n4_act.sem, n4_act.at(b, 1))
                    mean(bank[6][:, 0:T], sq4).then_inc(n4_pe.sem, 1)

                def run(a, f, g, nxt):
                    for c in range(FC + 2):
                        if f and c < FC:
                            gate(f, c)
                        if g and c == 0:
                            q_turn(g, 0)
                        if g and c == 6:
                            q_turn(g, 1)
                        if a and c < FC:
                            max_scores(a, 2 * c)
                            max_scores(a, 2 * c + 1)
                        if f and c >= 2:
                            ffn_out(f, c - 2)
                    if a:
                        max_turn(a)
                    if nxt:
                        if f:
                            pe.wait_ge(g_dve.sem, g_dve.at(f))
                        norm_a(nxt)
                    if g:
                        mlp_down(g)
                    if f:
                        norm_g(f)
                    for t in range(4):
                        if a:
                            for h in range(4 * t, 4 * t + 4):
                                scores(a, h)
                        if g:
                            (y_turn, adapter_down, adapter_up, ln_mean)[t](g)
                        if a:
                            if t == 2 and f:
                                pe.wait_ge(x2_dve.sem, x2_dve.at(f, DC))
                            attend(a, t)
                    if nxt:
                        project_qk(nxt)
                    if g:
                        ln_var(g)
                    if a:
                        project(a)
                    if nxt:
                        project_v(nxt)
                    if a:
                        norm_f(a)
                    if f:
                        for n in range(8):
                            up(f, n)

                pe.wait_ge(init_dve.sem, 5)
                norm_a(Batch(0))
                project_qk(Batch(0))
                project_v(Batch(0))
                whole(pe, run)

            @block.scalar
            def _(act):
                def square(dst, src, count):
                    act.activation(dst, src, ACT.Square).then_inc(count.sem, 1)

                def guess(y, bank_n, eps, count, b, k):
                    act.activation(y[:], bank[bank_n][:, 0:T], ACT.Ln, bias=eps).then_inc(count.sem, 1)
                    act.wait_ge(count.sem, count.at(b, k))
                    act.activation(y[:], y[:], ACT.Exp, scale=-0.5).then_inc(count.sem, 1)

                def square_a(b):
                    act.wait_ge(x_in_dma.sem, x_in_dma.at(b))
                    if b.follows():
                        act.wait_ge(v_mm.sem, v_mm.at(b, back=1))
                    square(h1[:], x_in[:], n1_act)

                def guess_a(b):
                    act.wait_ge(n1_pe.sem, n1_pe.at(b))
                    if b.follows():
                        act.wait_ge(n1_dve.sem, n1_dve.at(b, back=1))
                    guess(y1, 5, eps_rms, n1_act, b, 2)

                def split_qk(b):
                    if b.follows():
                        act.wait_ge(pv_mm.sem, pv_mm.at(b, back=1))
                    for x, done in ((0, q_mm), (1, k_mm)):
                        act.wait_ge(done.sem, done.at(b))
                        act.activation(qk_split[:, x, :, 0, :], halves(x), ACT.Copy).then_inc(qk_hi.sem, 1)

                def copy_v(b):
                    act.wait_ge(v_mm.sem, v_mm.at(b))
                    act.activation(v_aug[:, :, :, 0:DH], halves(2).rearrange("p t (h r) -> p t h r", r=DH), ACT.Copy)\
                        .then_inc(v_ready.sem, 1)

                def max_row_out(b):
                    act.wait_ge(max_t.sem, max_t.at(b))
                    if b.follows():
                        act.wait_ge(max_dma.sem, max_dma.at(b, back=1))
                    act.activation(max_rows, bank[0][0:H, 0:T], ACT.Copy).then_inc(max_row.sem, 1)

                def exps(b, h):
                    act.wait_ge(s_mm.sem, s_mm.at(b, h + 1))
                    if h == 0:
                        act.wait_ge(qk_dram_w.sem, qk_dram_w.at(b))
                    if h >= SLOTS:
                        act.wait_ge(pv_mm.sem, pv_mm.at(b, (h - SLOTS) // 4 + 1))
                    act.activation(probs[:, h % SLOTS], halves(h % 2), ACT.Exp, scale=float(H / D) ** 0.5).then_inc(s_exp.sem, 1)

                def den_guess(b, u):
                    act.wait_ge(o_dve.sem, o_dve.at(b, 4 * u + 1))
                    act.activation(den_y[:], den[:], ACT.Ln).then_inc(den_act.sem, 1)
                    act.wait_ge(den_act.sem, den_act.at(b, 2 * u + 1))
                    act.activation(den_y[:], den_y[:], ACT.Exp, scale=-1.0).then_inc(den_act.sem, 1)

                def square_f(b):
                    act.wait_ge(x1_dve.sem, x1_dve.at(b))
                    if b.follows():
                        act.wait_ge(n2_hi.sem, n2_hi.at(b, back=1))
                        act.wait_ge(n2_dve.sem, n2_dve.at(b, back=1))
                    square(h2[:], x1[:], n2_act)

                def guess_f(b):
                    act.wait_ge(n2_pe.sem, n2_pe.at(b))
                    guess(y2, 4, eps_rms, n2_act, b, 2)

                def hi_f(b):
                    act.wait_ge(n2_dve.sem, n2_dve.at(b, 6))
                    if b.follows():
                        act.wait_ge(g_mm.sem, g_mm.at(b, back=1))
                    act.activation(h2_hi[:], h2[:], ACT.Copy).then_inc(n2_hi.sem, 1)

                def silu(b, c):
                    act.wait_ge(g_mm.sem, g_mm.at(b, c + 1))
                    if b.follows() or c > 1:
                        act.wait_ge(g_dve.sem, g_dve.at(b, c - 1))
                    act.activation(silu_g[:, c % 2, :], halves(4 + c % 2)[:, 0, :], ACT.Silu).then_inc(g_silu.sem, 1)

                def act_high(b, c):
                    act.wait_ge(g_dve.sem, g_dve.at(b, c + 1))
                    if b.follows() or c > 2:
                        act.wait_ge(fo_mm.sem, fo_mm.at(b, c - 2))
                    act.activation(act_hi[:, c % 3, :], act_f[:, c % 2, :], ACT.Copy).then_inc(g_hi.sem, 1)

                def square_g(b):
                    act.wait_ge(x2_dve.sem, x2_dve.at(b))
                    if b.follows():
                        act.wait_ge(n3_hi.sem, n3_hi.at(b, back=1))
                        act.wait_ge(n3_dve.sem, n3_dve.at(b, back=1))
                    square(h3[:], x2_new[:], n3_act)

                def guess_g(b):
                    act.wait_ge(n3_pe.sem, n3_pe.at(b))
                    guess(y3, 4, eps_rms, n3_act, b, 2)

                def hi_g(b):
                    act.wait_ge(n3_dve.sem, n3_dve.at(b, 6))
                    if b.follows():
                        act.wait_ge(u_mm.sem, u_mm.at(b, back=1))
                    act.activation(h3_hi[:], h3[:], ACT.Copy).then_inc(n3_hi.sem, 1)

                def gelu(b, n):
                    act.wait_ge(u_mm.sem, u_mm.at(b, n + 1))
                    if b.follows() or n > 1:
                        act.wait_ge(u_dve.sem, u_dve.at(b, n - 1))
                    act.activation(gelu_g[:, n % 2, :], halves(6 + n % 2)[:, 1, :], ACT.Gelu).then_inc(u_gelu.sem, 1)

                def square_x(b):
                    act.wait_ge(n4_dve.sem, n4_dve.at(b, 2))
                    square(sq4, xc[:], n4_act)

                def guess_x(b):
                    act.wait_ge(n4_pe.sem, n4_pe.at(b))
                    if b.follows():
                        act.wait_ge(n4_dve.sem, n4_dve.at(b, back=1))
                    act.activation(y4[:], bank[6][:, 0:T], ACT.Ln, bias=eps_ln).then_inc(y4_ln.sem, 1)
                    act.wait_ge(y4_ln.sem, y4_ln.at(b))
                    act.activation(y4[:], y4[:], ACT.Exp, scale=-0.5).then_inc(n4_act.sem, 1)

                def run(a, f, g, nxt):
                    if nxt:
                        square_a(nxt)
                    if f:
                        act.preload_act_table_set("silu_and_others")
                        for c in range(FC + 1):
                            if c < FC:
                                silu(f, c)
                            if c >= 1:
                                act_high(f, c - 1)
                    act.preload_act_table_set("natural_log_exp_and_others")
                    if a:
                        max_row_out(a)
                    if nxt:
                        guess_a(nxt)
                    if f:
                        square_g(f)
                        guess_g(f)
                    for t in range(4):
                        if a:
                            for h in range(4 * t, 4 * t + 4):
                                exps(a, h)
                            if t == 2:
                                den_guess(a, 0)
                        if f and t == 1:
                            hi_g(f)
                        if f and t == 2:
                            act.wait_ge(x2_dve.sem, x2_dve.at(f))
                            if f.follows():
                                act.wait_ge(x3_dve.sem, x3_dve.at(f, back=1))
                            act.activation(x2[:], x2_new[:], ACT.Copy).then_inc(x2_cp.sem, 1)
                    if a:
                        den_guess(a, 1)
                    if nxt:
                        split_qk(nxt)
                    if g:
                        square_x(g)
                        guess_x(g)
                    if a:
                        square_f(a)
                    if nxt:
                        copy_v(nxt)
                    if a:
                        guess_f(a)
                    if f:
                        act.preload_act_table_set("gelu_and_others")
                    for n in range(8):
                        if f:
                            gelu(f, n)
                        if a and n == 2:
                            hi_f(a)

                act.preload_act_table_set("natural_log_exp_and_others")
                square_a(Batch(0))
                guess_a(Batch(0))
                split_qk(Batch(0))
                copy_v(Batch(0))
                whole(act, run)

            @block.vector
            def _(dve):
                def newton(b, y, n, eps, count, k):
                    v = bank[n][:, 0:T]
                    dve.scalar_tensor_tensor(v, v, eps, y[:], ALU.add, ALU.mult).then_inc(count.sem, 1)
                    dve.wait_ge(count.sem, count.at(b, k + 1))
                    dve.tensor_tensor(v, v, y[:], ALU.mult).then_inc(count.sem, 1)
                    dve.wait_ge(count.sem, count.at(b, k + 2))
                    dve.scalar_tensor_tensor(y[:], v, 3.0, y[:], ALU.subtract, ALU.mult).then_inc(count.sem, 1)
                    dve.wait_ge(count.sem, count.at(b, k + 3))

                def wide(y):
                    return y[:].rearrange("p (o t) -> p o t", o=1).broadcast_to([P, DC, T])

                def norm_a(b):
                    dve.wait_ge(n1_act.sem, n1_act.at(b))
                    newton(b, y1, 5, EPS_RMS, n1_dve, 0)
                    dve.tensor_tensor(h1[:], x_in[:], wide(y1), ALU.mult).then_inc(n1_dve.sem, 1)
                    dve.wait_ge(n1_dve.sem, n1_dve.at(b, 4))
                    for c in range(DC):
                        dve.tensor_scalar(h1[:, c, :], h1[:, c, :], par_a1[:, 0, c:c + 1], par_a1[:, 1, c:c + 1],
                                          ALU.mult, ALU.add).then_inc(n1_dve.sem, 1)

                def low_qk(b):
                    for x in range(2):
                        dve.wait_ge(qk_hi.sem, qk_hi.at(b, x + 1))
                        dve.tensor_tensor(qk_split[:, x, :, 1, :], halves(x), qk_split[:, x, :, 0, :].bitcast(F32), ALU.subtract)\
                            .then_inc(qk_lo.sem, 1)

                def row_max(b, n):
                    pair, qt = n // 2, n % 2
                    dve.wait_ge(max_mm.sem, max_mm.at(b, n + 1))
                    if n == 0:
                        if b.follows():
                            dve.wait_ge(max_t.sem, max_t.at(b, back=1))
                    dve.tensor_reduce(neg_max[:, qt, :, pair:pair + 1].rearrange("p a o -> p (a o)"), halves(n % 3), AX_X, ALU.max,
                                      negate=True).then_inc(max_red.sem, 1)

                def normalise(b, u):
                    dve.wait_ge(pv_mm.sem, pv_mm.at(b, 2 * u + 2))
                    k = 4 * u
                    if u == 0:
                        if b.follows():
                            dve.wait_ge(wo_mm.sem, wo_mm.at(b, back=1))
                            dve.wait_ge(o_dve.sem, o_dve.at(b, back=1))
                    else:
                        dve.wait_ge(o_dve.sem, o_dve.at(b, 4))
                    dve.tensor_copy(idle, eps_rms)
                    dve.stream_shuffle(den[:], halves(2 + u), [DH + i % DH for i in range(32)]).then_inc(o_dve.sem, 1)
                    dve.wait_ge(den_act.sem, den_act.at(b, 2 * u + 2))
                    dve.wait_ge(o_dve.sem, o_dve.at(b, k + 1))
                    dve.tensor_tensor(den[:], den[:], den_y[:], ALU.mult).then_inc(o_dve.sem, 1)
                    dve.wait_ge(o_dve.sem, o_dve.at(b, k + 2))
                    dve.scalar_tensor_tensor(den[:], den[:], 2.0, den_y[:], ALU.subtract, ALU.mult).then_inc(o_dve.sem, 1)
                    dve.wait_ge(o_dve.sem, o_dve.at(b, k + 3))
                    dve.tensor_tensor(o_norm[:, 2 * u:2 * u + 2, :], halves(2 + u), den[:], ALU.mult).then_inc(o_dve.sem, 1)

                def residual_1(b):
                    dve.wait_ge(wo_mm.sem, wo_mm.at(b))
                    dve.wait_ge(x_res_dma.sem, x_res_dma.at(b))
                    if b.follows():
                        dve.wait_ge(x2_dve.sem, x2_dve.at(b, back=1))
                    for c in range(DC):
                        dve.scalar_tensor_tensor(x1[:, c, :], halves(3)[:, c, :], par_a2[:, 0, c:c + 1], x_res[:, c, :],
                                                 ALU.mult, ALU.add).then_inc(x1_dve.sem, 1)

                def norm_f(b):
                    dve.wait_ge(n2_act.sem, n2_act.at(b))
                    newton(b, y2, 4, EPS_RMS, n2_dve, 0)
                    dve.tensor_tensor(h2[:], x1[:], wide(y2), ALU.mult).then_inc(n2_dve.sem, 1)
                    dve.wait_ge(n2_dve.sem, n2_dve.at(b, 4))
                    for c in range(DC):
                        dve.tensor_scalar(h2[:, c, :], h2[:, c, :], par_a2[:, 1, c:c + 1], par_a2[:, 2, c:c + 1],
                                          ALU.mult, ALU.add).then_inc(n2_dve.sem, 1)

                def low_f(b):
                    dve.wait_ge(n2_hi.sem, n2_hi.at(b))
                    if b.follows():
                        dve.wait_ge(g_mm.sem, g_mm.at(b, back=1))
                    dve.tensor_tensor(h2_lo[:], h2[:], h2_hi[:].bitcast(F32), ALU.subtract).then_inc(n2_dve.sem, 1)

                def gated(b, c):
                    dve.wait_ge(g_silu.sem, g_silu.at(b, c + 1))
                    if b.follows() or c > 1:
                        dve.wait_ge(g_lo.sem, g_lo.at(b, c - 1))
                    dve.tensor_tensor(act_f[:, c % 2, :], halves(4 + c % 2)[:, 1, :], silu_g[:, c % 2, :], ALU.mult)\
                        .then_inc(g_dve.sem, 1)

                def residual_2(b):
                    dve.wait_ge(fo_mm.sem, fo_mm.at(b))
                    dve.wait_ge(par_f_dma.sem, par_f_dma.at(b))
                    if b.follows():
                        dve.wait_ge(x2_cp.sem, x2_cp.at(b, back=1))
                        dve.wait_ge(n3_dve.sem, n3_dve.at(b, back=1))
                    for c in range(DC):
                        dve.tensor_scalar(x2_new[:, c, :], halves(3)[:, c, :], par_f[:, 0, c:c + 1], par_f[:, 1, c:c + 1],
                                          ALU.mult, ALU.add).then_inc(x2_dve.sem, 1)
                    dve.wait_ge(x2_dve.sem, x2_dve.at(b, 2))
                    for c in range(DC):
                        dve.tensor_tensor(x2_new[:, c, :], x2_new[:, c, :], x1[:, c, :], ALU.add).then_inc(x2_dve.sem, 1)

                def norm_g(b):
                    dve.wait_ge(n3_act.sem, n3_act.at(b))
                    newton(b, y3, 4, EPS_RMS, n3_dve, 0)
                    dve.tensor_tensor(h3[:], x2_new[:], wide(y3), ALU.mult).then_inc(n3_dve.sem, 1)
                    dve.wait_ge(n3_dve.sem, n3_dve.at(b, 4))
                    for c in range(DC):
                        dve.tensor_scalar(h3[:, c, :], h3[:, c, :], par_f[:, 2, c:c + 1], None, ALU.mult)\
                            .then_inc(n3_dve.sem, 1)

                def low_g(b):
                    dve.wait_ge(n3_hi.sem, n3_hi.at(b))
                    if b.follows():
                        dve.wait_ge(u_mm.sem, u_mm.at(b, back=1))
                    dve.tensor_tensor(h3_lo[:], h3[:], h3_hi[:].bitcast(F32), ALU.subtract).then_inc(n3_dve.sem, 1)

                def gated_u(b, n):
                    dve.wait_ge(u_gelu.sem, u_gelu.at(b, n + 1))
                    t, c = n // UC, n % UC
                    if c == 0 and b.follows():
                        dve.wait_ge(q_dve.sem, q_dve.at(b, 7 * t + 7, back=1))
                    dve.tensor_tensor(act_u[:, t, c * UW:(c + 1) * UW], halves(6 + n % 2)[:, 0, :], gelu_g[:, n % 2, :],
                                      ALU.mult).then_inc(u_dve.sem, 1)

                def quantise_max(b, t):
                    dve.wait_ge(u_dve.sem, u_dve.at(b, UC * t + UC))
                    m = slice(t, t + 1)
                    dve.tensor_reduce(q_max[:, m], act_u[:, t], AX_X, ALU.max, apply_absolute_value=True).then_inc(q_dve.sem, 1)

                def quantise_factors(b, t):
                    m, k = slice(t, t + 1), 7 * t
                    dve.wait_ge(q_dve.sem, q_dve.at(b, k + 1))
                    if b.follows():
                        dve.wait_ge(y_dve.sem, y_dve.at(b, back=1))
                    dve.tensor_scalar(q_clip[:, m], q_max[:, m], 1e-5, None, ALU.max).then_inc(q_dve.sem, 1)
                    dve.wait_ge(q_dve.sem, q_dve.at(b, k + 2))
                    dve.reciprocal(q_scale[:, m], q_clip[:, m]).then_inc(q_dve.sem, 1)
                    dve.tensor_scalar(q_back[:, m], q_clip[:, m], down_scale[:], 1.0 / 127.0, ALU.mult, ALU.mult)\
                        .then_inc(q_dve.sem, 1)
                    dve.wait_ge(q_dve.sem, q_dve.at(b, k + 4))
                    dve.tensor_scalar(q_scale[:, m], q_scale[:, m], 127.0, None, ALU.mult).then_inc(q_dve.sem, 1)

                def quantise_round(b, t):
                    m, k = slice(t, t + 1), 7 * t
                    dve.wait_ge(q_dve.sem, q_dve.at(b, k + 5))
                    dve.tensor_scalar(act_u[:, t], act_u[:, t], q_scale[:, m], MAGIC, ALU.mult, ALU.add).then_inc(q_dve.sem, 1)

                def quantise_int(b, t):
                    dve.wait_ge(q_dve.sem, q_dve.at(b, 7 * t + 6))
                    if t == 1:
                        dve.wait_ge(qT_mm.sem, qT_mm.at(b, 1))
                    if t == 0 and b.follows():
                        dve.wait_ge(qT_mm.sem, qT_mm.at(b, back=1))
                    dve.tensor_scalar(q_int[:], act_u[:, t], MAGIC, 127.0, ALU.subtract, ALU.min).then_inc(q_dve.sem, 1)

                quantise = (quantise_max, quantise_factors, quantise_round, quantise_int)

                def q_turned(b, t):
                    dve.wait_ge(qT_mm.sem, qT_mm.at(b, t + 1))
                    if b.follows():
                        dve.wait_ge(d_mm.sem, d_mm.at(b, back=1))
                    dve.tensor_scalar(q_T[:, t].rearrange("p c n -> p (c n)"), bank[7 - t][:].bitcast(BF16), -128.0, None, ALU.max)\
                        .then_inc(qT_dve.sem, 1)

                def scaled_y(b):
                    dve.wait_ge(d_mm.sem, d_mm.at(b))
                    if b.follows():
                        dve.wait_ge(yT_mm.sem, yT_mm.at(b, back=1))
                    for t in range(TT):
                        dve.tensor_scalar(mlp_y[:, t, :], halves(7)[:, t, :], q_back[:, t:t + 1], None, ALU.mult)\
                            .then_inc(y_dve.sem, 1)

                def residual_3(b):
                    dve.wait_ge(yT_mm.sem, yT_mm.at(b))
                    dve.wait_ge(x2_cp.sem, x2_cp.at(b))
                    if b.follows():
                        dve.wait_ge(n4_dve.sem, n4_dve.at(b, 2, back=1))
                    dve.tensor_tensor(x3[:], halves(6), x2[:], ALU.add).then_inc(x3_dve.sem, 1)

                def relu(b):
                    dve.wait_ge(ad_mm.sem, ad_mm.at(b))
                    if b.follows():
                        dve.wait_ge(au_mm.sem, au_mm.at(b, back=1))
                    dve.tensor_scalar(adapt_h[:], bank[7][:, 0:T], bd_c[:], 0.0, ALU.add, ALU.max).then_inc(ad_h.sem, 1)

                def residual_4(b):
                    dve.wait_ge(au_mm.sem, au_mm.at(b))
                    for c in range(DC):
                        dve.scalar_tensor_tensor(x3[:, c, :], halves(6)[:, c, :], bu_c[:, c:c + 1], x3[:, c, :], ALU.add, ALU.add)\
                            .then_inc(x4_dve.sem, 1)

                def centre(b):
                    dve.wait_ge(n4_pe.sem, n4_pe.at(b, 1))
                    if b.follows():
                        dve.wait_ge(out_dma.sem, out_dma.at(b, back=1))
                    m = bank[7][:, 0:T]
                    for c in range(DC):
                        dve.tensor_tensor(xc[:, c, :], x3[:, c, :], m, ALU.subtract).then_inc(n4_dve.sem, 1)

                def layer_norm(b):
                    dve.wait_ge(n4_act.sem, n4_act.at(b))
                    newton(b, y4, 6, EPS_LN, n4_dve, 2)
                    for c in range(DC):
                        dve.scalar_tensor_tensor(xc[:, c, :], xc[:, c, :], neg_w2[:, c:c + 1], y4[:], ALU.mult, ALU.mult)\
                            .then_inc(x5_dve.sem, 1)
                    dve.wait_ge(x5_dve.sem, x5_dve.at(b))
                    for c in range(DC):
                        dve.tensor_scalar(xc[:, c, :], xc[:, c, :], par_g[:, c:c + 1], None, ALU.add).then_inc(n4_dve.sem, 1)

                def run(a, f, g, nxt):
                    for c in range(FC):
                        if f:
                            gated(f, c)
                        if a:
                            row_max(a, 2 * c)
                            row_max(a, 2 * c + 1)
                        if g and 1 <= c <= 4:
                            quantise[c - 1](g, 1)
                        if g and c == 1:
                            q_turned(g, 0)
                    if g:
                        q_turned(g, 1)
                    if f:
                        residual_2(f)
                    if nxt:
                        norm_a(nxt)
                    if g:
                        scaled_y(g)
                    if f:
                        norm_g(f)
                    if g:
                        residual_3(g)
                    if f:
                        low_g(f)
                    if g:
                        relu(g)
                    if a:
                        normalise(a, 0)
                    if g:
                        residual_4(g)
                        centre(g)
                    if a:
                        normalise(a, 1)
                    if nxt:
                        low_qk(nxt)
                    if g:
                        layer_norm(g)
                    if a:
                        residual_1(a)
                        norm_f(a)
                    for n in range(8):
                        if f:
                            gated_u(f, n)
                            if n >= UC:
                                quantise[n - UC](f, 0)
                        if a and n == 1:
                            low_f(a)

                dve.memset(k_stack[:].bitcast(F32), 0.0).then_inc(init_dve.sem, 1)
                dve.memset(q_stack[:].bitcast(F32), 0.0).then_inc(init_dve.sem, 1)
                dve.memset(zero_row, 0.0).then_inc(init_dve.sem, 1)
                dve.memset(one_row, 1.0).then_inc(init_dve.sem, 1)
                dve.memset(v_aug[:], 1.0).then_inc(init_dve.sem, 1)
                dve.wait_ge(init_dve.sem, 5)
                norm_a(Batch(0))
                low_qk(Batch(0))
                whole(dve, run)


_OUT = (NB, D, T)


def kernel(**inputs):
    import numpy as np
    import concourse.bacc as bacc
    from concourse.bass_utils import run_bass_kernel_spmd

    v = {k: np.asarray(a) for k, a in inputs.items()}
    t = lambda name: v[name].T
    wdd = v["L2_cond_Wdd"].reshape(BN, D, C).transpose(2, 1, 0).reshape(C, D * BN)
    wdu = v["L2_cond_Wdu"].reshape(D, BN, C).transpose(2, 1, 0).reshape(C, D * BN)

    def chunked(a):
        return a.reshape(DC, P, BN).transpose(1, 0, 2).reshape(P, DC * BN)

    arrays = {
        "xT": v["x"].transpose(0, 2, 1),
        "condT": t("cond_256"),
        "w_cond": np.concatenate([t(n) for n in (
            "L0_cond_attn_gamma_w", "L0_cond_attn_beta_w", "L0_cond_attn_alpha_w", "L0_cond_ffn_gamma_w",
            "L0_cond_ffn_beta_w", "L0_cond_ffn_alpha_w", "L1_cond_norm_w", "L3_cond_lin_w")], axis=1),
        "w_qkvT": np.concatenate([t("L0_cond_W_q"), t("L0_cond_W_k"), t("L0_cond_W_v")], axis=1),
        "w_oT": t("L0_cond_W_o"),
        "w_ghT": np.concatenate([t("L0_cond_gate_w"), t("L0_cond_hidden_w")], axis=1),
        "w_outT": t("L0_cond_out_w"),
        "out_b": v["L0_cond_out_b"].reshape(DC, P).T,
        "w_upT": t("L1_cond_up_w"),
        "w_downT": t("L1_cond_down_w"),
        "w_hyper": np.concatenate([wdd, wdu], axis=0),
        "adapt_w": np.concatenate([chunked(t("L2_cond_Wd")), t("L2_cond_Wu")], axis=1),
        "adapt_b": np.concatenate([chunked(v["L2_cond_bdd"].reshape(BN, D).T), v["L2_cond_bdu"].reshape(D, BN).T], axis=1),
        "bd": v["L2_cond_bd"].reshape(BN, 1),
        "bu": v["L2_cond_bu"].reshape(DC, P).T,
        "ln_w": v["L3_cond_weight"].reshape(DC, P).T,
        "ln_b": v["L3_cond_bias"].reshape(DC, P).T,
        "lin_b": v["L3_cond_lin_b"].reshape(DC, P).T,
        "ident_in": np.eye(P, dtype=np.float32),
    }
    arrays = {k: np.ascontiguousarray(a) for k, a in arrays.items()}
    nc = bacc.Bacc("TRN2", target_bir_lowering=False, num_devices=1)
    args = {k: nc.dram_tensor(k, a.shape, mybir.dt.from_np(a.dtype), kind="ExternalInput").ap() for k, a in arrays.items()}
    out = nc.dram_tensor("out", _OUT, F32, kind="ExternalOutput").ap()
    build(nc, **args, out=out)
    r = run_bass_kernel_spmd(nc, [arrays], core_ids=[0])
    return np.asarray(r.results[0]["out"]).transpose(0, 2, 1)
```

```python
from contextlib import ExitStack

import concourse.bass as bass
from concourse import mybir

F32 = mybir.dt.float32
F32R = mybir.dt.float32r
BF16 = mybir.dt.bfloat16
ALU = mybir.AluOpType
ACT = mybir.ActivationFunctionType
AX_X = mybir.AxisListType.X

P = 128
NB, T, D = 16, 256, 256
C = 64
DC = D // P
TT = T // P
H, DH = 16, 16
NPAIR = H // 2
F = 1024
FC = F // P
UC = 4
UW = F // UC
BN = 128
SLOTS = 7
NHY, HYW = 16, 2048
MAGIC = 12582912.0
EPS_RMS, EPS_LN = 1e-6, 1e-5

A_GAMMA, A_BETA, NEG_ALPHA, F_GAMMA, F_BETA, F_ALPHA, ALPHA_B, L1_SCALE, OFFSET = range(9)
NPAR = 9


class Batch:

    def __init__(self, i, off=0):
        self.i, self.off = i, off

    def of(self, mul, add=0):
        return self.i * mul + (self.off * mul + add)

    def follows(self):
        return not isinstance(self.i, int) or self.i + self.off > 0


class Count:

    def __init__(self, sem, per=1):
        self.sem, self.per = sem, per

    def at(self, batch, k=None, back=0):
        return batch.of(self.per, (self.per if k is None else k) - back * self.per)


def known(eng, value):
    if not isinstance(value, int):
        eng.compute_val(value)
    return value


def build(nc, xT, condT, w_cond, w_qkvT, w_oT, w_ghT, w_outT, out_b, w_upT, w_downT,
          w_hyper, head_rows, adapt_w, adapt_b, bd, bu, ln_w, ln_b, lin_b, ident_in, out):
    with ExitStack() as ctx:
        def sb(name, shape, dt=F32, stack=ctx):
            return stack.enter_context(nc.sbuf_tensor(name, shape, dt))

        def sem(name, per=1):
            return Count(ctx.enter_context(nc.semaphore(name)), per)

        bank = [ctx.enter_context(nc.psum_tensor(f"bank{i}", [P, 512], F32)) for i in range(8)]

        def halves(i):
            return bank[i][:].rearrange("p (a n) -> p a n", a=2)

        q_dram = nc.dram_tensor("q_dram", [H * DH, 2, T], F32, kind="Internal").ap()
        k_dram = nc.dram_tensor("k_dram", [H * DH, 2, T], F32, kind="Internal").ap()
        cond_dram = nc.dram_tensor("cond_dram", [NB, P, NPAR * DC], F32, kind="Internal").ap()
        delta_dram = nc.dram_tensor("delta_dram", [NHY * HYW // 512, 2 * NB, 512], F32, kind="Internal").ap()

        w_qkv = sb("w_qkv", [P, DC, 3 * D])
        w_o = sb("w_o", [P, DC, D])
        rows_of = sb("rows_of", [P, 2])
        gh_hi = sb("gh_hi", [P, DC, 2 * F], F32R)
        fo_hi = sb("fo_hi", [P, FC, D], F32R)
        with ExitStack() as early:
            w_early = sb("w_early", [P, 2, 2048], stack=early)
        up_hi = sb("up_hi", [P, DC, 2 * F], F32R)
        cond_w = w_early[0:C, 0, :]
        w_down = w_early[:, 1, :]
        with ExitStack() as early:
            w_raw = sb("w_raw", [P, 5, 2048], stack=early)
        gh_lo = sb("gh_lo", [P, DC, 2 * F], F32R)
        fo_lo = sb("fo_lo", [P, FC, D], F32R)
        up_lo = sb("up_lo", [P, DC, 2 * F], F32R)
        down = sb("down", [P, FC, D], BF16)
        adapt_base = sb("adapt_base", [P, 512])
        ident = sb("ident", [P, P])
        ident_bf = sb("ident_bf", [P, P], BF16)
        mean_w = sb("mean_w", [P, P])
        down_scale = sb("down_scale", [P, 1])
        bd_c = sb("bd_c", [P, 1])
        bu_c = sb("bu_c", [P, DC])
        ln_w_c = sb("ln_w_c", [P, DC])
        neg_w2 = sb("neg_w2", [P, DC])
        columns = sb("columns", [P, 4])
        eps_rms, eps_ln, idle, pool_idle = (columns[:, i:i + 1] for i in range(4))

        x_in = sb("x_in", [P, DC, T])
        x_res = sb("x_res", [P, DC, T])
        x1 = sb("x1", [P, DC, T])
        par_a1 = sb("par_a1", [P, 2, DC])
        par_a2 = sb("par_a2", [P, 3, DC])
        h1 = sb("h1", [P, DC, T])
        y1 = sb("y1", [P, T])
        k_stack = sb("k_stack", [P, H, T], F32R)
        q_stack = sb("q_stack", [P, NPAIR, T], F32R)
        few_rows = sb("few_rows", [P, T])
        max_rows = few_rows[0:H, :].bitcast(F32R)
        zero_row = few_rows[32:32 + NPAIR, :]
        one_row = few_rows[64:64 + NPAIR, :]
        v_aug = sb("v_aug", [P, TT, H, 2 * DH])
        probs = sb("probs", [P, SLOTS, TT, T])
        qk_split = probs[:, 0:4].rearrange("p s k t -> p (s k t)").bitcast(F32R)\
            .rearrange("p (x t l n) -> p x t l n", x=2, t=2, l=2)
        neg_max = sb("neg_max", [P, TT, 2, NPAIR])
        den_raw = sb("den_raw", [P, T])
        den = sb("den", [P, T])
        den_y = sb("den_y", [P, T])
        den_x = sb("den_x", [P, T])
        o_norm = sb("o_norm", [P, DC, T])
        h2 = sb("h2", [P, DC, T])
        h2_lo = sb("h2_lo", [P, DC, T], F32R)
        y2 = sb("y2", [P, T])
        h2_hi = sb("h2_hi", [P, DC, T], F32R)
        par_f = sb("par_f", [P, 3, DC])
        par_g = sb("par_g", [P, DC])

        with ExitStack() as st:
            hyper = sb("hyper", [P, 4, HYW], stack=st)
            hyper_s = sb("hyper_s", [P, 4, 512], stack=st)
            cond_t = sb("cond_t", [P, 2 * NB], stack=st)
            par = sb("par", [P, NPAR, DC, NB], stack=st)
            par_t = sb("par_t", [P, NB, NPAR, DC], stack=st)
            vectors = sb("vectors", [P, 3, DC], stack=st)
            out_b_c, lin_b_c, ln_b_c = (vectors[:, i] for i in range(3))
            tanh_t = sb("tanh_t", [P, DC, NB], stack=st)
            adapt_bias = sb("adapt_bias", [P, 512], stack=st)
            w_stats = sb("w_stats", [P, 3], stack=st)
            w_abs, w_mean, w_rec = (w_stats[:, i:i + 1] for i in range(3))
            ones = sb("ones", [P, P], stack=st)
        raw = [(w_ghT[0:P, :], gh_hi[:, 0, :], gh_lo[:, 0, :]),
               (w_ghT[P:D, :], gh_hi[:, 1, :], gh_lo[:, 1, :]),
               (w_outT.rearrange("(c p) n -> p c n", p=P), fo_hi[:].rearrange("p c n -> p (c n)"),
                fo_lo[:].rearrange("p c n -> p (c n)")),
               (w_upT[0:P, :], up_hi[:, 0, :], up_lo[:, 0, :]),
               (w_upT[P:D, :], up_hi[:, 1, :], up_lo[:, 1, :])]
        NRAW = len(raw)

        silu_g = sb("silu_g", [P, 2, T])
        act_f = sb("act_f", [P, 2, T])
        act_hi = sb("act_hi", [P, 3, T], F32R)
        act_lo = sb("act_lo", [P, 3, T], F32R)
        x2_new = sb("x2_new", [P, DC, T])
        h3 = sb("h3", [P, DC, T])
        h3_lo = sb("h3_lo", [P, DC, T], F32R)
        y3 = sb("y3", [P, T])
        h3_hi = sb("h3_hi", [P, DC, T], F32R)
        x2 = sb("x2", [P, DC, T])
        gelu_g = sb("gelu_g", [P, 2, UW])
        act_u = sb("act_u", [P, TT, F])
        q_max = sb("q_max", [P, TT])
        q_clip = sb("q_clip", [P, TT])
        q_scale = sb("q_scale", [P, TT])
        q_back = sb("q_back", [P, TT])
        q_int = sb("q_int", [P, F], BF16)
        q_T = sb("q_T", [P, TT, FC, P], BF16)
        mlp_y = sb("mlp_y", [P, TT, D])
        x3 = sb("x3", [P, DC, T])
        adapt = sb("adapt", [P, 512])
        adapt_h = sb("adapt_h", [P, T])
        xc = sb("xc", [P, DC, T])
        sq4 = adapt[:].rearrange("p (c t) -> p c t", c=DC)
        y4 = sb("y4", [P, T])

        x_in_dma, x_res_dma = sem("x_in_dma", 32), sem("x_res_dma", 32)
        qk_dram_w, stack_dma = sem("qk_dram_w", 32), sem("stack_dma", 16 * 14)
        max_dma = sem("max_dma", 32)
        par_f_dma, adapt_dma, out_dma = sem("par_f_dma", 16), sem("adapt_dma", 64), sem("out_dma", 16)
        n1_act, n1_pe, n1_dve = sem("n1_act", 3), sem("n1_pe"), sem("n1_dve", 6)
        n2_act, n2_pe, n2_dve, n2_hi = sem("n2_act", 3), sem("n2_pe"), sem("n2_dve", 7), sem("n2_hi")
        n3_act, n3_pe, n3_dve, n3_hi = sem("n3_act", 3), sem("n3_pe"), sem("n3_dve", 7), sem("n3_hi")
        n4_act, n4_pe, n4_dve = sem("n4_act", 2), sem("n4_pe", 2), sem("n4_dve", 5)
        q_mm, k_mm, v_mm = sem("q_mm"), sem("k_mm"), sem("v_mm", TT)
        qk_hi, qk_lo, v_ready = sem("qk_hi", 2), sem("qk_lo", 2), sem("v_ready", 2)
        max_mm, max_red = sem("max_mm", 16), sem("max_red", 16)
        max_t, max_row = sem("max_t"), sem("max_row")
        s_mm, s_exp, pv_mm = sem("s_mm", 16), sem("s_exp", 16), sem("pv_mm", 4)
        den_act, o_dve = sem("den_act", 4), sem("o_dve", 16)
        wo_mm, x1_dve = sem("wo_mm"), sem("x1_dve", 2)
        g_mm, g_silu, g_dve, g_hi, g_lo = (sem(n, FC) for n in ("g_mm", "g_silu", "g_dve", "g_hi", "g_lo"))
        fo_mm, x2_dve = sem("fo_mm", FC), sem("x2_dve", 4)
        u_mm, u_gelu, u_dve = sem("u_mm", 8), sem("u_gelu", 8), sem("u_dve", 8)
        q_dve, qT_mm, qT_dve = sem("q_dve", 14), sem("qT_mm", 2), sem("qT_dve", 2)
        d_mm, y_dve, yT_mm, x3_dve, x2_cp = sem("d_mm", TT), sem("y_dve", 2), sem("yT_mm"), sem("x3_dve"), sem("x2_cp")
        adapt_w_ready, ad_mm, ad_h, au_mm, x4_dve = (sem("adapt_w_ready"), sem("ad_mm"), sem("ad_h"), sem("au_mm"),
                                                     sem("x4_dve", 2))
        y4_ln, x5_pool = sem("y4_ln"), sem("x5_pool", 4)
        cond_in, vec_in, small_in, qkv_in, wo_in = sem("cond_in"), sem("vec_in"), sem("small_in"), sem("qkv_in"), sem("wo_in")
        raw_in = [sem(f"raw_in{i}") for i in range(NRAW)]
        down_in, cond_mm, cond_out, init_dma = sem("down_in"), sem("cond_mm"), sem("cond_out"), sem("init_dma")
        blank, consts, init_dve, init_pool = sem("blank"), sem("consts"), sem("init_dve"), sem("init_pool")
        par_ready = sem("par_ready")
        tanh_act, table, ternary, abs_mm = sem("tanh_act"), sem("table"), sem("ternary"), sem("abs_mm")
        w_hi, w_lo = sem("w_hi"), sem("w_lo")
        hyper_in = [sem(f"hyper_in{i}") for i in range(4)]
        hyper_mm, hyper_ev = sem("hyper_mm"), sem("hyper_ev")
        hyper_out = [sem(f"hyper_out{i}") for i in range(4)]
        TABLE = 9 + 3 * DC
        LOW_FROM = 6
        TERNARY = 4 + 3 * 4

        def rows(t):
            return t.rearrange("(c p) t -> p c t", p=P)

        def bat(b):
            return b.of(1)

        def batch_of(tensor, b):
            return tensor[bass.ds(bat(b), 1)].rearrange("o a b -> (o a) b")

        def whole(eng, run):
            run(Batch(0), None, None, Batch(1))
            run(Batch(1), Batch(0), None, Batch(2))
            run(Batch(2), Batch(1), Batch(0), Batch(3))
            with eng.Fori(3, NB - 1) as i:
                run(Batch(i), Batch(i, -1), Batch(i, -2), Batch(i, 1))
            run(Batch(NB - 1), Batch(NB - 2), Batch(NB - 3), None)
            run(None, Batch(NB - 1), Batch(NB - 2), None)
            run(None, None, Batch(NB - 1), None)

        def starts(b):
            return b is not None and not b.follows()

        with nc.Block() as block:

            @block.sync
            def _(sp):
                def load_x(b):
                    if b.follows():
                        sp.wait_ge(n1_dve.sem, n1_dve.at(b, back=1))
                    sp.dma_start(x_in[:], rows(batch_of(xT, b))).then_inc(x_in_dma.sem, 16)
                    sp.dma_start(par_a1[:].rearrange("p k c -> p (k c)"),
                                 batch_of(cond_dram, b)[:, A_GAMMA * DC:(A_BETA + 1) * DC]).then_inc(x_in_dma.sem, 16)

                def stack_qk(b):
                    for x, dram in enumerate((q_dram, k_dram)):
                        hi_value = known(sp, qk_hi.at(b, x + 1))
                        lo_value = known(sp, qk_lo.at(b, x + 1))
                        if b.follows():
                            left_value = known(sp, stack_dma.at(b, back=1))
                            sp.wait_ge(stack_dma.sem, left_value)
                        sp.wait_ge(qk_hi.sem, hi_value)
                        sp.wait_ge(qk_lo.sem, lo_value)
                        sp.dma_start(dram.rearrange("(t p) l n -> p t (l n)", p=P),
                                     qk_split[:, x].rearrange("p t l n -> p t (l n)").bitcast(F32)).then_inc(qk_dram_w.sem, 16)
                    if b.follows():
                        sp.wait_ge(s_mm.sem, s_mm.at(b, back=1))
                    for a in range(2):
                        sp.dma_start(q_stack[64 * a + 48:64 * a + 49, :, :].bitcast(F32), zero_row).then_inc(stack_dma.sem, 16)
                    sp.wait_ge(qk_dram_w.sem, qk_dram_w.at(b))
                    for dram, dst, parts in ((q_dram, q_stack, (0, 1, 0)), (k_dram, k_stack, (0, 0, 1))):
                        for a in range(2):
                            for c, part in enumerate(parts):
                                src = dram[:, part].rearrange("(m a r) n -> a r m n", a=2, r=DH)[a]
                                at = 64 * a + DH * c
                                to = dst[at:at + DH, :, :] if dst is q_stack else \
                                    dst[at:at + DH].rearrange("r (m a) n -> r a m n", a=2)[:, a]
                                sp.dma_start(to.bitcast(F32), src).then_inc(stack_dma.sem, 16)

                def load_res(b):
                    if b.follows():
                        res_value = known(sp, x1_dve.at(b, back=1))
                        par_value = known(sp, n2_dve.at(b, back=1))
                        sp.wait_ge(x1_dve.sem, res_value)
                        sp.wait_ge(n2_dve.sem, par_value)
                    sp.dma_start(x_res[:], rows(batch_of(xT, b))).then_inc(x_res_dma.sem, 16)
                    sp.dma_start(par_a2[:].rearrange("p k c -> p (k c)"),
                                 batch_of(cond_dram, b)[:, NEG_ALPHA * DC:(F_BETA + 1) * DC]).then_inc(x_res_dma.sem, 16)

                def run(a, f, g, nxt):
                    if nxt:
                        load_x(nxt)
                    if a:
                        load_res(a)
                    if f:
                        if f.follows():
                            sp.wait_ge(n3_dve.sem, n3_dve.at(f, back=1))
                        sp.dma_start(par_f[:].rearrange("p k c -> p (k c)"),
                                     batch_of(cond_dram, f)[:, F_ALPHA * DC:(L1_SCALE + 1) * DC]).then_inc(par_f_dma.sem, 16)
                    if g:
                        if starts(g):
                            for s in range(4):
                                sp.wait_ge(hyper_out[s].sem, 16 * NHY // 4)
                            sp.wait_ge(hyper_mm.sem, NHY)
                        else:
                            adapt_value = known(sp, au_mm.at(g, back=1))
                            par_value = known(sp, x5_pool.at(g, back=1))
                            sp.wait_ge(au_mm.sem, adapt_value)
                            sp.wait_ge(x5_pool.sem, par_value)
                        for c in range(DC):
                            sp.dma_start(adapt[:, c * BN:(c + 1) * BN],
                                         delta_dram[:, bass.ds(bat(g), 1), :][c * P // 4:(c + 1) * P // 4]
                                         .rearrange("m o (q n) -> m (o q) n", n=BN)).then_inc(adapt_dma.sem, 16)
                        sp.dma_start(adapt[:, 256:512],
                                     delta_dram[:, bass.ds(g.of(1, NB), 1), :][0:P // 2]
                                     .rearrange("m o (q n) -> m (o q) n", n=D)).then_inc(adapt_dma.sem, 16)
                        sp.dma_start(par_g[:], batch_of(cond_dram, g)[:, OFFSET * DC:(OFFSET + 1) * DC])\
                            .then_inc(adapt_dma.sem, 16)
                    if a:
                        row_value = known(sp, max_row.at(a))
                        mm_value = known(sp, max_mm.at(a))
                        sp.wait_ge(max_row.sem, row_value)
                        sp.wait_ge(max_mm.sem, mm_value)
                        for par in range(2):
                            sp.dma_start(q_stack[64 * par + 48:64 * par + 49, :, :].bitcast(F32),
                                         max_rows[NPAIR * par:NPAIR * (par + 1), :].bitcast(F32)).then_inc(max_dma.sem, 16)
                    if nxt:
                        stack_qk(nxt)
                    if g:
                        sp.wait_ge(x5_pool.sem, x5_pool.at(g))
                        sp.dma_start(rows(batch_of(out, g)), xc[:]).then_inc(out_dma.sem, 16)

                for c in range(DC):
                    sp.dma_start(x_in[:, c, :], rows(batch_of(xT, Batch(0)))[:, c, :]).then_inc(x_in_dma.sem, 16)
                sp.wait_ge(blank.sem, 1)
                sp.dma_start(cond_t[0:C, 0:NB], condT).then_inc(cond_in.sem, 16)
                sp.dma_start(cond_t[C:P, NB:2 * NB], condT).then_inc(cond_in.sem, 16)
                sp.dma_start(cond_w, w_cond).then_inc(cond_in.sem, 16)
                for dst, src in ((ln_w_c[:], ln_w), (lin_b_c, lin_b), (ln_b_c, ln_b), (out_b_c, out_b)):
                    sp.dma_start(dst, src).then_inc(vec_in.sem, 16)
                sp.dma_start(w_qkv[:], w_qkvT.rearrange("(c p) n -> p c n", p=P)).then_inc(qkv_in.sem, 16)
                for dst, src in ((ident, ident_in), (rows_of, head_rows), (bd_c, bd), (bu_c, bu), (adapt_base, adapt_w), (adapt_bias, adapt_b)):
                    sp.dma_start(dst[:], src).then_inc(small_in.sem, 16)
                sp.dma_start(w_down.rearrange("p (c n) -> p c n", n=D), w_downT.rearrange("(c p) n -> p c n", p=P))\
                    .then_inc(down_in.sem, 16)
                sp.wait_ge(init_pool.sem, 2)
                sp.wait_ge(init_dve.sem, 4)
                for a in range(2):
                    sp.dma_start(k_stack[64 * a + 48:64 * a + 49].rearrange("r (m a) n -> r a m n", a=2)[:, a].bitcast(F32),
                                 one_row).then_inc(init_dma.sem, 16)
                sp.wait_ge(table.sem, TABLE - 1)
                sp.dma_start(cond_dram.rearrange("b p k -> p b k"),
                             par_t[:].rearrange("p b k c -> p b (k c)")).then_inc(cond_out.sem, 16)
                sp.dma_start(w_o[:], w_oT.rearrange("(c p) n -> p c n", p=P)).then_inc(wo_in.sem, 16)
                sp.wait_ge(init_dma.sem, 32)
                stack_qk(Batch(0))
                sp.wait_ge(cond_out.sem, 16)
                whole(sp, run)
                sp.wait_ge(out_dma.sem, 16 * NB)

            @block.gpsimd
            def _(pool):
                def layer_out(b):
                    pool.wait_ge(adapt_dma.sem, adapt_dma.at(b))
                    pool.wait_ge(n4_dve.sem, n4_dve.at(b))
                    pool.tensor_tensor(xc[:], xc[:], y4[:].rearrange("p (o t) -> p o t", o=1).broadcast_to([P, DC, T]), ALU.mult)\
                        .then_inc(x5_pool.sem, 1)
                    pool.wait_ge(x5_pool.sem, x5_pool.at(b, 1))
                    pool.tensor_tensor(pool_idle, pool_idle, pool_idle, ALU.mult).then_inc(x5_pool.sem, 1)
                    for c in range(DC):
                        pool.tensor_scalar(xc[:, c, :], xc[:, c, :], neg_w2[:, c:c + 1], par_g[:, c:c + 1], ALU.mult, ALU.add)\
                            .then_inc(x5_pool.sem, 1)

                def run(a, f, g, nxt):
                    if f:
                        for c in range(FC):
                            pool.wait_ge(g_hi.sem, g_hi.at(f, c + 1))
                            if f.follows() or c > 2:
                                pool.wait_ge(fo_mm.sem, fo_mm.at(f, c - 2))
                            pool.tensor_tensor(act_lo[:, c % 3, :], act_f[:, c % 2, :], act_hi[:, c % 3, :].bitcast(F32),
                                               ALU.subtract).then_inc(g_lo.sem, 1)
                    if g:
                        if starts(g):
                            pool.wait_ge(table.sem, TABLE)
                            pool.wait_ge(consts.sem, 6)
                            pool.wait_ge(init_pool.sem, 1)
                        pool.wait_ge(adapt_dma.sem, adapt_dma.at(g))
                        pool.tensor_tensor(adapt[:], adapt[:], adapt_base[:], ALU.add).then_inc(adapt_w_ready.sem, 1)
                        layer_out(g)

                def hyper_load(n):
                    if n >= 4:
                        pool.wait_ge(hyper_mm.sem, n - 3)
                    pool.dma_start(hyper[:, n % 4, :], w_hyper[:, n * HYW:(n + 1) * HYW]).then_inc(hyper_in[n % 4].sem, 16)

                hyper_load(0)
                pool.memset(pool_idle, 0.0).then_inc(init_pool.sem, 1)
                pool.memset(k_stack[:].bitcast(F32), 0.0).then_inc(init_pool.sem, 1)
                for n in range(1, NHY):
                    hyper_load(n)
                    if LOW_FROM <= n < LOW_FROM + NRAW:
                        _, hi, lo = raw[n - LOW_FROM]
                        pool.wait_ge(w_hi.sem, n - LOW_FROM + 1)
                        pool.tensor_tensor(lo, w_raw[:, n - LOW_FROM, :], hi.bitcast(F32), ALU.subtract).then_inc(w_lo.sem, 1)
                whole(pool, run)

            @block.tensor
            def _(pe):
                def mean(at, src):
                    for c in range(DC):
                        mm = pe.matmul(at, mean_w[:], src[:, c, :], start=(c == 0), stop=(c == DC - 1))
                    return mm

                def norm_a(b):
                    pe.wait_ge(n1_act.sem, n1_act.at(b, 1))
                    mean(bank[4][:, 0:T], h1).then_inc(n1_pe.sem, 1)

                def project_qk(b):
                    pe.wait_ge(n1_dve.sem, n1_dve.at(b))
                    if b.follows():
                        pe.wait_ge(s_exp.sem, s_exp.at(b, back=1))
                    for x, done in ((0, q_mm), (1, k_mm)):
                        for t in range(2):
                            for c in range(DC):
                                mm = pe.matmul(halves(x)[:, t, :], w_qkv[:, c, x * D + t * P:x * D + (t + 1) * P], h1[:, c, :],
                                               start=(c == 0), stop=(c == DC - 1))
                        mm.then_inc(done.sem, 1)

                def project_v(b, t):
                    if t == 0 and b.follows():
                        pe.wait_ge(o_dve.sem, o_dve.at(b, 5, back=1))
                    for c in range(DC):
                        mm = pe.matmul(halves(2)[:, t, :], h1[:, c, t * P:(t + 1) * P], w_qkv[:, c, 2 * D:3 * D],
                                       start=(c == 0), stop=(c == DC - 1))
                    mm.then_inc(v_mm.sem, 1)

                def max_scores(b, n):
                    pair, qt = n // 2, n % 2
                    if n == 0:
                        pe.wait_ge(stack_dma.sem, stack_dma.at(b))
                    if n == 0:
                        pe.wait_ge(qk_lo.sem, qk_lo.at(b, 1))
                    if n == 1:
                        pe.wait_ge(qk_lo.sem, qk_lo.at(b, 2))
                    if n == 2:
                        pe.wait_ge(v_ready.sem, v_ready.at(b))
                    if n >= 3:
                        pe.wait_ge(max_red.sem, max_red.at(b, n - 2))
                    pe.matmul(bank[n % 3][:], q_stack[:, pair, qt * P:(qt + 1) * P],
                              k_stack[:, 2 * pair:2 * pair + 2, :], start=True, stop=True).then_inc(max_mm.sem, 1)

                def max_turn(b):
                    pe.wait_ge(max_red.sem, max_red.at(b))
                    for t in range(TT):
                        mm = pe.transpose(bank[0][0:H, t * P:(t + 1) * P], neg_max[:, t].rearrange("p a m -> p (a m)"), ident[:])
                    mm.then_inc(max_t.sem, 1)

                def scores(b, h):
                    if h == 0:
                        pe.wait_ge(max_dma.sem, max_dma.at(b))
                        pe.wait_ge(max_row.sem, max_row.at(b))
                    if h >= 2:
                        pe.wait_ge(s_exp.sem, s_exp.at(b, h - 1))
                    for k in range(TT):
                        mm = pe.matmul(halves(h % 2)[:, k, :], k_stack[:, h, k * P:(k + 1) * P], q_stack[:, h // 2, :],
                                       start=True, stop=True)
                    mm.then_inc(s_mm.sem, 1)

                def attend(b, t):
                    pe.wait_ge(s_exp.sem, s_exp.at(b, 4 * t + 4))
                    pe.wait_ge(v_ready.sem, v_ready.at(b))
                    at = halves(2 + t // 2)
                    for k in range(TT):
                        for j in range(4):
                            mm = pe.matmul(at[32 * j:32 * j + 32, t % 2, :], v_aug[:, k, 4 * t + j, :], probs[:, (4 * t + j) % SLOTS, k, :],
                                           start=(k == 0), stop=(k == TT - 1), tile_position=(0, 32 * j))
                    mm.then_inc(pv_mm.sem, 1)

                def project(b):
                    pe.wait_ge(o_dve.sem, o_dve.at(b))
                    for m in range(DC):
                        for c in range(DC):
                            mm = pe.matmul(halves(3)[:, m, :], w_o[:, c, m * P:(m + 1) * P], o_norm[:, c, :],
                                           start=(c == 0), stop=(c == DC - 1))
                    mm.then_inc(wo_mm.sem, 1)

                def norm_f(b):
                    pe.wait_ge(n2_act.sem, n2_act.at(b, 1))
                    if b.follows():
                        pe.wait_ge(g_dve.sem, g_dve.at(b, back=1))
                    mean(bank[4][:, 0:T], h2[:]).then_inc(n2_pe.sem, 1)

                def gate(b, c):
                    if c == 0:
                        pe.wait_ge(n2_dve.sem, n2_dve.at(b))
                        pe.wait_ge(n2_hi.sem, n2_hi.at(b))
                    if c >= 2:
                        pe.wait_ge(g_dve.sem, g_dve.at(b, c - 1))
                    at = halves(4 + c % 2)
                    for x in range(2):
                        n = 0
                        for w, h in ((gh_hi, h2_hi), (gh_lo, h2_hi), (gh_hi, h2_lo)):
                            for d in range(DC):
                                mm = pe.matmul(at[:, x, :], w[:, d, x * F + c * P:x * F + (c + 1) * P], h[:, d, :],
                                               start=(n == 0), stop=(n == 5))
                                n += 1
                    mm.then_inc(g_mm.sem, 1)

                def ffn_out(b, c):
                    pe.wait_ge(g_lo.sem, g_lo.at(b, c + 1))
                    if c == 0:
                        pe.wait_ge(x1_dve.sem, x1_dve.at(b))
                    for m in range(DC):
                        for n, (w, h) in enumerate(((fo_hi, act_hi), (fo_lo, act_hi), (fo_hi, act_lo))):
                            mm = pe.matmul(halves(3)[:, m, :], w[:, c, m * P:(m + 1) * P], h[:, c % 3, :],
                                           start=(c == 0 and m == 0 and n == 0), stop=(c == FC - 1 and n == 2),
                                           skip_group_check=True)
                    mm.then_inc(fo_mm.sem, 1)

                def norm_g(b):
                    pe.wait_ge(n3_act.sem, n3_act.at(b, 1))
                    mean(bank[5][:, 0:T], h3[:]).then_inc(n3_pe.sem, 1)

                def up(b, n):
                    t, c = n // UC, n % UC
                    if n == 0:
                        pe.wait_ge(n3_dve.sem, n3_dve.at(b))
                        pe.wait_ge(n3_hi.sem, n3_hi.at(b))
                        if b.follows():
                            pe.wait_ge(n4_dve.sem, n4_dve.at(b, 2, back=1))
                    if n == 1 and b.follows():
                        pe.wait_ge(n4_dve.sem, n4_dve.at(b, 5, back=1))
                    if n >= 2:
                        pe.wait_ge(u_dve.sem, u_dve.at(b, n - 1))
                    at = halves(7 - n % 2)
                    for x in range(2):
                        i = 0
                        for w, h in ((up_hi, h3_hi), (up_lo, h3_hi), (up_hi, h3_lo)):
                            for d in range(DC):
                                mm = pe.matmul(at[:, x, :], h[:, d, t * P:(t + 1) * P],
                                               w[:, d, x * F + c * UW:x * F + (c + 1) * UW], start=(i == 0), stop=(i == 5))
                                i += 1
                    mm.then_inc(u_mm.sem, 1)

                def q_turn(b, t):
                    pe.wait_ge(q_dve.sem, q_dve.at(b, 7 * t + 7))
                    at = bank[7 - t][:].bitcast(BF16).rearrange("p (c n) -> p c n", n=P)
                    if t == 1:
                        pe.wait_ge(u_dve.sem, u_dve.at(b))
                    for c in range(FC):
                        mm = pe.transpose(at[:, c, :], q_int[:, c * P:(c + 1) * P], ident_bf[:])
                    mm.then_inc(qT_mm.sem, 1)

                def mlp_down(b, t):
                    pe.wait_ge(u_dve.sem, u_dve.at(b))
                    pe.wait_ge(qT_dve.sem, qT_dve.at(b))
                    for c in range(FC):
                        mm = pe.matmul(halves(7)[:, t, :], q_T[:, t, c, :], down[:, c, :], start=(c == 0), stop=(c == FC - 1))
                    mm.then_inc(d_mm.sem, 1)

                def y_turn(b):
                    pe.wait_ge(y_dve.sem, y_dve.at(b))
                    for m in range(DC):
                        for t in range(TT):
                            mm = pe.transpose(halves(6)[:, m, t * P:(t + 1) * P], mlp_y[:, t, m * P:(m + 1) * P], ident[:])
                    mm.then_inc(yT_mm.sem, 1)

                def adapter_down(b):
                    pe.wait_ge(adapt_w_ready.sem, adapt_w_ready.at(b))
                    pe.wait_ge(x3_dve.sem, x3_dve.at(b))
                    for c in range(DC):
                        mm = pe.matmul(bank[7][:, 0:T], adapt[:, c * BN:(c + 1) * BN], x3[:, c, :], start=(c == 0), stop=(c == DC - 1))
                    mm.then_inc(ad_mm.sem, 1)

                def adapter_up(b):
                    pe.wait_ge(ad_h.sem, ad_h.at(b))
                    for m in range(DC):
                        mm = pe.matmul(halves(6)[:, m, :], adapt[:, 256 + m * P:256 + (m + 1) * P], adapt_h[:], start=True, stop=True)
                    mm.then_inc(au_mm.sem, 1)

                def ln_mean(b):
                    pe.wait_ge(x4_dve.sem, x4_dve.at(b))
                    mean(bank[7][:, 0:T], x3).then_inc(n4_pe.sem, 1)

                def ln_var(b):
                    pe.wait_ge(n4_act.sem, n4_act.at(b, 1))
                    mean(bank[6][:, 0:T], sq4).then_inc(n4_pe.sem, 1)

                def hyper_product(n):
                    pe.wait_ge(hyper_in[n % 4].sem, 16 * (n // 4 + 1))
                    if n >= 2:
                        pe.wait_ge(hyper_ev.sem, n - 1)
                    for j in range(4):
                        mm = pe.matmul(bank[6 + n % 2][32 * j:32 * j + 32, :], cond_t[:],
                                       hyper[:, n % 4, j * 512:(j + 1) * 512], start=True, stop=True,
                                       tile_position=(0, 32 * j))
                    mm.then_inc(hyper_mm.sem, 1)

                def run(a, f, g, nxt):
                    if starts(f):
                        pe.wait_ge(abs_mm.sem, 1)
                        pe.wait_ge(ternary.sem, TERNARY)
                        pe.wait_ge(w_hi.sem, NRAW)
                        pe.wait_ge(w_lo.sem, NRAW)
                        pe.wait_ge(hyper_ev.sem, NHY)
                        pe.wait_ge(small_in.sem, 16 * 6)
                    for c in range(FC + 2):
                        if f and c < FC:
                            gate(f, c)
                        if g and c == 1:
                            q_turn(g, 0)
                        if g and c == 6:
                            q_turn(g, 1)
                        if a and c < FC:
                            max_scores(a, 2 * c)
                            max_scores(a, 2 * c + 1)
                        if a and c == FC:
                            if starts(a):
                                pe.wait_ge(small_in.sem, 16 * 6)
                            max_turn(a)
                        if nxt and c == FC:
                            if f:
                                pe.wait_ge(g_dve.sem, g_dve.at(f, 7))
                            norm_a(nxt)
                        if f and c >= 2:
                            ffn_out(f, c - 2)
                        if starts(a) and c in (1, 3, 5, 7):
                            hyper_product(4 + c // 2)
                    if starts(a):
                        hyper_product(8)
                    if g:
                        mlp_down(g, 0)
                    if a:
                        scores(a, 0)
                        scores(a, 1)
                    if g:
                        mlp_down(g, 1)
                    if f:
                        norm_g(f)
                    if a:
                        scores(a, 2)
                        scores(a, 3)
                    for t in range(4):
                        if g and t < 3:
                            (y_turn, adapter_down, adapter_up)[t](g)
                        if a:
                            if t < 3:
                                scores(a, 4 * t + 4)
                                scores(a, 4 * t + 5)
                            if t == 2 and f:
                                pe.wait_ge(x2_dve.sem, x2_dve.at(f, DC))
                            attend(a, t)
                            if t < 3:
                                scores(a, 4 * t + 6)
                                scores(a, 4 * t + 7)
                        if starts(a):
                            hyper_product(9 + t)
                    if nxt:
                        project_qk(nxt)
                    if g:
                        ln_mean(g)
                    if starts(a):
                        hyper_product(13)
                    if a:
                        if starts(a):
                            pe.wait_ge(wo_in.sem, 16)
                        project(a)
                    if g:
                        ln_var(g)
                    if nxt:
                        project_v(nxt, 0)
                    if starts(a):
                        hyper_product(14)
                    if a:
                        norm_f(a)
                    if nxt:
                        project_v(nxt, 1)
                    if starts(a):
                        hyper_product(15)
                    if f:
                        for n in range(8):
                            up(f, n)

                pe.wait_ge(consts.sem, 4)
                norm_a(Batch(0))
                pe.wait_ge(cond_in.sem, 48)
                for m in range(8):
                    for c in range(DC):
                        mm = pe.matmul(bank[5][:, (m * DC + c) * NB:(m * DC + c + 1) * NB],
                                       cond_w[:, m * D + c * P:m * D + (c + 1) * P], cond_t[0:C, 0:NB],
                                       start=True, stop=True)
                mm.then_inc(cond_mm.sem, 1)
                hyper_product(0)
                pe.wait_ge(qkv_in.sem, 16)
                project_qk(Batch(0))
                project_v(Batch(0), 0)
                project_v(Batch(0), 1)
                for n in range(1, 4):
                    hyper_product(n)
                pe.wait_ge(table.sem, TABLE - 1)
                pe.wait_ge(ternary.sem, 1)
                pe.matmul(bank[5][:, 0:1], ones[:], w_abs, start=True, stop=True).then_inc(abs_mm.sem, 1)
                whole(pe, run)

            @block.scalar
            def _(act):
                def square(dst, src, count):
                    act.activation(dst, src, ACT.Square).then_inc(count.sem, 1)

                def guess(y, bank_n, eps, count, b, k):
                    act.activation(y[:], bank[bank_n][:, 0:T], ACT.Ln, bias=eps).then_inc(count.sem, 1)
                    act.wait_ge(count.sem, count.at(b, k))
                    act.activation(y[:], y[:], ACT.Exp, scale=-0.5).then_inc(count.sem, 1)

                def square_a(b):
                    act.wait_ge(x_in_dma.sem, x_in_dma.at(b))
                    if b.follows():
                        act.wait_ge(v_mm.sem, v_mm.at(b, back=1))
                    square(h1[:], x_in[:], n1_act)

                def guess_a(b):
                    act.wait_ge(n1_pe.sem, n1_pe.at(b))
                    if b.follows():
                        act.wait_ge(n1_dve.sem, n1_dve.at(b, back=1))
                    guess(y1, 4, eps_rms, n1_act, b, 2)

                def split_qk(b):
                    if b.follows():
                        act.wait_ge(pv_mm.sem, pv_mm.at(b, back=1))
                    for x, done in ((0, q_mm), (1, k_mm)):
                        act.wait_ge(done.sem, done.at(b))
                        act.activation(qk_split[:, x, :, 0, :], halves(x), ACT.Copy).then_inc(qk_hi.sem, 1)

                def copy_v(b):
                    act.wait_ge(v_mm.sem, v_mm.at(b))
                    to = v_aug[:].rearrange("p k h w -> p (k h) w").rearrange("p (c a j) w -> p c a j w", a=2, j=4)
                    at = bank[2][:].rearrange("p (c a j r) -> p c a j r", a=2, j=4, r=DH)
                    for a in range(2):
                        act.activation(to[:, :, a, :, DH * a:DH * (a + 1)], at[:, :, a], ACT.Copy).then_inc(v_ready.sem, 1)

                def max_row_out(b):
                    act.wait_ge(max_t.sem, max_t.at(b))
                    if b.follows():
                        act.wait_ge(max_dma.sem, max_dma.at(b, back=1))
                    act.activation(max_rows, bank[0][0:H, 0:T], ACT.Copy).then_inc(max_row.sem, 1)

                def exps(b, h):
                    act.wait_ge(s_mm.sem, s_mm.at(b, h + 1))
                    if h == 0:
                        act.wait_ge(qk_dram_w.sem, qk_dram_w.at(b))
                    if h >= SLOTS:
                        act.wait_ge(pv_mm.sem, pv_mm.at(b, (h - SLOTS) // 4 + 1))
                    act.activation(probs[:, h % SLOTS], halves(h % 2), ACT.Exp, scale=float(H / D) ** 0.5).then_inc(s_exp.sem, 1)

                def den_guess(b, u):
                    act.wait_ge(o_dve.sem, o_dve.at(b, 8 * u + 3))
                    act.activation(den_y[:], den[:], ACT.Ln).then_inc(den_act.sem, 1)
                    act.wait_ge(den_act.sem, den_act.at(b, 2 * u + 1))
                    act.activation(den_y[:], den_y[:], ACT.Exp, scale=-1.0).then_inc(den_act.sem, 1)

                def square_f(b):
                    act.wait_ge(x1_dve.sem, x1_dve.at(b))
                    if b.follows():
                        act.wait_ge(n2_hi.sem, n2_hi.at(b, back=1))
                        act.wait_ge(n2_dve.sem, n2_dve.at(b, back=1))
                    square(h2[:], x1[:], n2_act)

                def guess_f(b):
                    act.wait_ge(n2_pe.sem, n2_pe.at(b))
                    guess(y2, 4, eps_rms, n2_act, b, 2)

                def hi_f(b):
                    act.wait_ge(n2_dve.sem, n2_dve.at(b, 6))
                    if b.follows():
                        act.wait_ge(g_mm.sem, g_mm.at(b, back=1))
                    act.activation(h2_hi[:], h2[:], ACT.Copy).then_inc(n2_hi.sem, 1)

                def silu(b, c):
                    act.wait_ge(g_mm.sem, g_mm.at(b, c + 1))
                    if b.follows() or c > 1:
                        act.wait_ge(g_dve.sem, g_dve.at(b, c - 1))
                    act.activation(silu_g[:, c % 2, :], halves(4 + c % 2)[:, 0, :], ACT.Silu).then_inc(g_silu.sem, 1)

                def act_high(b, c):
                    act.wait_ge(g_dve.sem, g_dve.at(b, c + 1))
                    if b.follows() or c > 2:
                        act.wait_ge(fo_mm.sem, fo_mm.at(b, c - 2))
                    act.activation(act_hi[:, c % 3, :], act_f[:, c % 2, :], ACT.Copy).then_inc(g_hi.sem, 1)

                def square_g(b):
                    act.wait_ge(x2_dve.sem, x2_dve.at(b))
                    if b.follows():
                        act.wait_ge(n3_hi.sem, n3_hi.at(b, back=1))
                        act.wait_ge(n3_dve.sem, n3_dve.at(b, back=1))
                    square(h3[:], x2_new[:], n3_act)

                def guess_g(b):
                    act.wait_ge(n3_pe.sem, n3_pe.at(b))
                    guess(y3, 5, eps_rms, n3_act, b, 2)

                def keep_x2(b):
                    act.wait_ge(x2_dve.sem, x2_dve.at(b))
                    if b.follows():
                        act.wait_ge(x3_dve.sem, x3_dve.at(b, back=1))
                    act.activation(x2[:], x2_new[:], ACT.Copy).then_inc(x2_cp.sem, 1)

                def hi_g(b):
                    act.wait_ge(n3_dve.sem, n3_dve.at(b, 6))
                    if b.follows():
                        act.wait_ge(u_mm.sem, u_mm.at(b, back=1))
                    act.activation(h3_hi[:], h3[:], ACT.Copy).then_inc(n3_hi.sem, 1)

                def gelu(b, n):
                    act.wait_ge(u_mm.sem, u_mm.at(b, n + 1))
                    if b.follows() or n > 1:
                        act.wait_ge(u_dve.sem, u_dve.at(b, n - 1))
                    act.activation(gelu_g[:, n % 2, :], halves(7 - n % 2)[:, 1, :], ACT.Gelu).then_inc(u_gelu.sem, 1)

                def square_x(b):
                    act.wait_ge(n4_dve.sem, n4_dve.at(b, 2))
                    square(sq4, xc[:], n4_act)

                def guess_x(b):
                    act.wait_ge(n4_pe.sem, n4_pe.at(b))
                    if b.follows():
                        act.wait_ge(x5_pool.sem, x5_pool.at(b, 1, back=1))
                    act.activation(y4[:], bank[6][:, 0:T], ACT.Ln, bias=eps_ln).then_inc(y4_ln.sem, 1)
                    act.wait_ge(y4_ln.sem, y4_ln.at(b))
                    act.activation(y4[:], y4[:], ACT.Exp, scale=-0.5).then_inc(n4_act.sem, 1)

                def hyper_out_piece(n):
                    act.wait_ge(hyper_mm.sem, n + 1)
                    if n >= 4:
                        act.wait_ge(hyper_out[n % 4].sem, 16 * (n // 4))
                    act.activation(hyper_s[:, n % 4, :], bank[6 + n % 2][:], ACT.Copy, scale=0.1).then_inc(hyper_ev.sem, 1)
                    act.wait_ge(hyper_ev.sem, n + 1)
                    act.dma_start(delta_dram[4 * n:4 * n + 4].rearrange("g r n -> (g r) n"), hyper_s[:, n % 4, :])\
                        .then_inc(hyper_out[n % 4].sem, 16)

                def raw_load(n):
                    src, dst = raw[n][0], w_raw[:, n, :]
                    if len(src.shape) == 3:
                        dst = dst.rearrange("p (c n) -> p c n", n=D)
                    act.dma_start(dst, src).then_inc(raw_in[n].sem, 16)

                def high_part(n):
                    act.wait_ge(raw_in[n].sem, 16)
                    if n >= 3:
                        act.wait_ge(cond_mm.sem, 1)
                        act.wait_ge(ternary.sem, TERNARY)
                    act.activation(raw[n][1], w_raw[:, n, :], ACT.Copy).then_inc(w_hi.sem, 1)

                def run(a, f, g, nxt):
                    if starts(a):
                        act.wait_ge(stack_dma.sem, stack_dma.at(a))
                        for n in range(2, NRAW):
                            raw_load(n)
                        for n in range(4, 8):
                            hyper_out_piece(n)
                            if n > 4:
                                high_part(n - 3)
                    if starts(f):
                        for s in range(4):
                            act.wait_ge(hyper_out[s].sem, 16 * NHY // 4)
                    if f:
                        act.preload_act_table_set("silu_and_others")
                    for c in range(FC + 1):
                        if f and c < FC:
                            silu(f, c)
                        if nxt and c == 1:
                            square_a(nxt)
                        if f and c >= 1:
                            act_high(f, c - 1)
                    if a:
                        max_row_out(a)
                    act.preload_act_table_set("natural_log_exp_and_others")
                    if nxt:
                        guess_a(nxt)
                    if f:
                        square_g(f)
                    if starts(a):
                        hyper_out_piece(8)
                    for t in range(4):
                        for h in range(4 * t, 4 * t + 4):
                            if a:
                                exps(a, h)
                            if f and h == 3:
                                guess_g(f)
                            if f and h == 9:
                                hi_g(f)
                        if starts(a) and t > 0:
                            hyper_out_piece(8 + t)
                    if a:
                        den_guess(a, 0)
                    if f:
                        keep_x2(f)
                    if a:
                        den_guess(a, 1)
                    if starts(a):
                        hyper_out_piece(12)
                    if nxt:
                        split_qk(nxt)
                    if starts(a):
                        hyper_out_piece(13)
                    if g:
                        square_x(g)
                    if a:
                        square_f(a)
                    if g:
                        guess_x(g)
                    if starts(a):
                        hyper_out_piece(14)
                    if a:
                        guess_f(a)
                    if starts(a):
                        hyper_out_piece(15)
                    if f:
                        act.preload_act_table_set("gelu_and_others")
                    for n in range(8):
                        if f:
                            gelu(f, n)
                        if nxt and n == 1:
                            copy_v(nxt)
                        if a and n == 2:
                            hi_f(a)

                act.preload_act_table_set("natural_log_exp_and_others")
                act.wait_ge(x_in_dma.sem, 32)
                square(h1[:], x_in[:], n1_act)
                act.wait_ge(consts.sem, 4)
                guess_a(Batch(0))
                act.wait_ge(cond_mm.sem, 1)
                act.wait_ge(vec_in.sem, 64)
                for c in range(DC):
                    act.activation(tanh_t[:, c, :], bank[5][:, (14 + c) * NB:(15 + c) * NB], ACT.Tanh,
                                   bias=lin_b_c[:, c:c + 1]).then_inc(tanh_act.sem, 1)
                act.preload_act_table_set("natural_log_exp_and_others")
                hyper_out_piece(0)
                raw_load(0)
                raw_load(1)
                split_qk(Batch(0))
                act.wait_ge(init_dve.sem, 4)
                copy_v(Batch(0))
                hyper_out_piece(1)
                high_part(0)
                hyper_out_piece(2)
                high_part(1)
                hyper_out_piece(3)
                whole(act, run)

            @block.vector
            def _(dve):
                def newton(b, y, n, eps, count, k):
                    v = bank[n][:, 0:T]
                    dve.scalar_tensor_tensor(v, v, eps, y[:], ALU.add, ALU.mult).then_inc(count.sem, 1)
                    dve.wait_ge(count.sem, count.at(b, k + 1))
                    dve.tensor_tensor(v, v, y[:], ALU.mult).then_inc(count.sem, 1)
                    dve.wait_ge(count.sem, count.at(b, k + 2))
                    dve.scalar_tensor_tensor(y[:], v, 3.0, y[:], ALU.subtract, ALU.mult).then_inc(count.sem, 1)
                    dve.wait_ge(count.sem, count.at(b, k + 3))

                def wide(y):
                    return y[:].rearrange("p (o t) -> p o t", o=1).broadcast_to([P, DC, T])

                def norm_a(b):
                    dve.wait_ge(n1_act.sem, n1_act.at(b))
                    newton(b, y1, 4, EPS_RMS, n1_dve, 0)
                    dve.tensor_tensor(h1[:], x_in[:], wide(y1), ALU.mult).then_inc(n1_dve.sem, 1)
                    dve.wait_ge(n1_dve.sem, n1_dve.at(b, 4))
                    for c in range(DC):
                        dve.tensor_scalar(h1[:, c, :], h1[:, c, :], par_a1[:, 0, c:c + 1], par_a1[:, 1, c:c + 1],
                                          ALU.mult, ALU.add).then_inc(n1_dve.sem, 1)

                def low_qk(b):
                    for x in range(2):
                        dve.wait_ge(qk_hi.sem, qk_hi.at(b, x + 1))
                        dve.tensor_tensor(qk_split[:, x, :, 1, :], halves(x), qk_split[:, x, :, 0, :].bitcast(F32), ALU.subtract)\
                            .then_inc(qk_lo.sem, 1)

                def row_max(b, n):
                    pair, qt = n // 2, n % 2
                    dve.wait_ge(max_mm.sem, max_mm.at(b, n + 1))
                    if n == 0:
                        if b.follows():
                            dve.wait_ge(max_t.sem, max_t.at(b, back=1))
                    dve.tensor_reduce(neg_max[:, qt, :, pair:pair + 1].rearrange("p a o -> p (a o)"), halves(n % 3), AX_X, ALU.max,
                                      negate=True).then_inc(max_red.sem, 1)

                def normalise(b, u):
                    k = 8 * u
                    even, odd = rows_of[:, 0:1], rows_of[:, 1:2]
                    tile, num = halves(2 + u), o_norm[:, u, :]
                    dve.wait_ge(pv_mm.sem, pv_mm.at(b, 2 * u + 2))
                    if u == 1:
                        dve.wait_ge(o_dve.sem, o_dve.at(b, 8))
                    if u == 0 and b.follows():
                        dve.wait_ge(wo_mm.sem, wo_mm.at(b, back=1))
                        dve.wait_ge(o_dve.sem, o_dve.at(b, back=1))
                    dve.tensor_scalar(den_raw[:], tile[:, 0, :], odd, None, ALU.mult).then_inc(o_dve.sem, 1)
                    dve.wait_ge(o_dve.sem, o_dve.at(b, k + 1))
                    dve.scalar_tensor_tensor(den_raw[:], tile[:, 1, :], even, den_raw[:], ALU.mult, ALU.add).then_inc(o_dve.sem, 1)
                    dve.wait_ge(o_dve.sem, o_dve.at(b, k + 2))
                    dve.tensor_copy(idle, eps_rms)
                    dve.stream_shuffle(den[:], den_raw[:], [(DH + i) % 32 for i in range(32)]).then_inc(o_dve.sem, 1)
                    dve.tensor_scalar(num, tile[:, 0, :], even, None, ALU.mult).then_inc(o_dve.sem, 1)
                    dve.wait_ge(o_dve.sem, o_dve.at(b, k + 4))
                    dve.scalar_tensor_tensor(num, tile[:, 1, :], odd, num, ALU.mult, ALU.add).then_inc(o_dve.sem, 1)

                def normalised(b, u):
                    k, num = 8 * u, o_norm[:, u, :]
                    dve.wait_ge(den_act.sem, den_act.at(b, 2 * u + 2))
                    dve.wait_ge(o_dve.sem, o_dve.at(b, k + 5))
                    dve.tensor_tensor(den_x[:], den[:], den_y[:], ALU.mult).then_inc(o_dve.sem, 1)
                    dve.wait_ge(o_dve.sem, o_dve.at(b, k + 6))
                    dve.scalar_tensor_tensor(den_x[:], den_x[:], 2.0, den_y[:], ALU.subtract, ALU.mult).then_inc(o_dve.sem, 1)
                    dve.wait_ge(o_dve.sem, o_dve.at(b, k + 7))
                    dve.tensor_tensor(num, num, den_x[:], ALU.mult).then_inc(o_dve.sem, 1)

                def residual_1(b):
                    dve.wait_ge(wo_mm.sem, wo_mm.at(b))
                    dve.wait_ge(x_res_dma.sem, x_res_dma.at(b))
                    if b.follows():
                        dve.wait_ge(x2_dve.sem, x2_dve.at(b, back=1))
                    for c in range(DC):
                        dve.scalar_tensor_tensor(x1[:, c, :], halves(3)[:, c, :], par_a2[:, 0, c:c + 1], x_res[:, c, :],
                                                 ALU.mult, ALU.add).then_inc(x1_dve.sem, 1)

                def norm_f(b):
                    dve.wait_ge(n2_act.sem, n2_act.at(b))
                    newton(b, y2, 4, EPS_RMS, n2_dve, 0)

                def scaled_f(b):
                    dve.tensor_tensor(h2[:], x1[:], wide(y2), ALU.mult).then_inc(n2_dve.sem, 1)
                    dve.wait_ge(n2_dve.sem, n2_dve.at(b, 4))
                    for c in range(DC):
                        dve.tensor_scalar(h2[:, c, :], h2[:, c, :], par_a2[:, 1, c:c + 1], par_a2[:, 2, c:c + 1],
                                          ALU.mult, ALU.add).then_inc(n2_dve.sem, 1)

                def low_f(b):
                    dve.wait_ge(n2_hi.sem, n2_hi.at(b))
                    if b.follows():
                        dve.wait_ge(g_mm.sem, g_mm.at(b, back=1))
                    dve.tensor_tensor(h2_lo[:], h2[:], h2_hi[:].bitcast(F32), ALU.subtract).then_inc(n2_dve.sem, 1)

                def gated(b, c):
                    dve.wait_ge(g_silu.sem, g_silu.at(b, c + 1))
                    if b.follows() or c > 1:
                        dve.wait_ge(g_lo.sem, g_lo.at(b, c - 1))
                    dve.tensor_tensor(act_f[:, c % 2, :], halves(4 + c % 2)[:, 1, :], silu_g[:, c % 2, :], ALU.mult)\
                        .then_inc(g_dve.sem, 1)

                def residual_2(b):
                    dve.wait_ge(fo_mm.sem, fo_mm.at(b))
                    dve.wait_ge(par_f_dma.sem, par_f_dma.at(b))
                    if b.follows():
                        dve.wait_ge(x2_cp.sem, x2_cp.at(b, back=1))
                        dve.wait_ge(n3_dve.sem, n3_dve.at(b, back=1))
                    for c in range(DC):
                        dve.tensor_scalar(x2_new[:, c, :], halves(3)[:, c, :], par_f[:, 0, c:c + 1], par_f[:, 1, c:c + 1],
                                          ALU.mult, ALU.add).then_inc(x2_dve.sem, 1)
                    dve.wait_ge(x2_dve.sem, x2_dve.at(b, 2))
                    for c in range(DC):
                        dve.tensor_tensor(x2_new[:, c, :], x2_new[:, c, :], x1[:, c, :], ALU.add).then_inc(x2_dve.sem, 1)

                def norm_g(b):
                    dve.wait_ge(n3_act.sem, n3_act.at(b))
                    newton(b, y3, 5, EPS_RMS, n3_dve, 0)
                    dve.tensor_tensor(h3[:], x2_new[:], wide(y3), ALU.mult).then_inc(n3_dve.sem, 1)
                    dve.wait_ge(n3_dve.sem, n3_dve.at(b, 4))
                    for c in range(DC):
                        dve.tensor_scalar(h3[:, c, :], h3[:, c, :], par_f[:, 2, c:c + 1], None, ALU.mult)\
                            .then_inc(n3_dve.sem, 1)

                def low_g(b):
                    dve.wait_ge(n3_hi.sem, n3_hi.at(b))
                    if b.follows():
                        dve.wait_ge(u_mm.sem, u_mm.at(b, back=1))
                    dve.tensor_tensor(h3_lo[:], h3[:], h3_hi[:].bitcast(F32), ALU.subtract).then_inc(n3_dve.sem, 1)

                def gated_u(b, n):
                    dve.wait_ge(u_gelu.sem, u_gelu.at(b, n + 1))
                    t, c = n // UC, n % UC
                    if c == 0 and b.follows():
                        dve.wait_ge(q_dve.sem, q_dve.at(b, 7 * t + 7, back=1))
                    dve.tensor_tensor(act_u[:, t, c * UW:(c + 1) * UW], halves(7 - n % 2)[:, 0, :], gelu_g[:, n % 2, :],
                                      ALU.mult).then_inc(u_dve.sem, 1)

                def quantise_max(b, t):
                    dve.wait_ge(u_dve.sem, u_dve.at(b, UC * t + UC))
                    m = slice(t, t + 1)
                    dve.tensor_reduce(q_max[:, m], act_u[:, t], AX_X, ALU.max, apply_absolute_value=True).then_inc(q_dve.sem, 1)

                def quantise_factors(b, t):
                    m, k = slice(t, t + 1), 7 * t
                    dve.wait_ge(q_dve.sem, q_dve.at(b, k + 1))
                    if b.follows():
                        dve.wait_ge(y_dve.sem, y_dve.at(b, back=1))
                    dve.tensor_scalar(q_clip[:, m], q_max[:, m], 1e-5, None, ALU.max).then_inc(q_dve.sem, 1)
                    dve.wait_ge(q_dve.sem, q_dve.at(b, k + 2))
                    dve.reciprocal(q_scale[:, m], q_clip[:, m]).then_inc(q_dve.sem, 1)
                    dve.tensor_scalar(q_back[:, m], q_clip[:, m], down_scale[:], 1.0 / 127.0, ALU.mult, ALU.mult)\
                        .then_inc(q_dve.sem, 1)
                    dve.wait_ge(q_dve.sem, q_dve.at(b, k + 4))
                    dve.tensor_scalar(q_scale[:, m], q_scale[:, m], 127.0, None, ALU.mult).then_inc(q_dve.sem, 1)

                def quantise_round(b, t):
                    m, k = slice(t, t + 1), 7 * t
                    dve.wait_ge(q_dve.sem, q_dve.at(b, k + 5))
                    dve.tensor_scalar(act_u[:, t], act_u[:, t], q_scale[:, m], MAGIC, ALU.mult, ALU.add).then_inc(q_dve.sem, 1)

                def quantise_int(b, t):
                    dve.wait_ge(q_dve.sem, q_dve.at(b, 7 * t + 6))
                    if t == 1:
                        dve.wait_ge(qT_mm.sem, qT_mm.at(b, 1))
                    if t == 0 and b.follows():
                        dve.wait_ge(qT_mm.sem, qT_mm.at(b, back=1))
                    dve.tensor_scalar(q_int[:], act_u[:, t], MAGIC, 127.0, ALU.subtract, ALU.min).then_inc(q_dve.sem, 1)

                quantise = (quantise_max, quantise_factors, quantise_round, quantise_int)

                def q_turned(b, t):
                    dve.wait_ge(qT_mm.sem, qT_mm.at(b, t + 1))
                    if b.follows():
                        dve.wait_ge(d_mm.sem, d_mm.at(b, back=1))
                    dve.tensor_scalar(q_T[:, t].rearrange("p c n -> p (c n)"), bank[7 - t][:].bitcast(BF16), -128.0, None, ALU.max)\
                        .then_inc(qT_dve.sem, 1)

                def scaled_y(b):
                    dve.wait_ge(d_mm.sem, d_mm.at(b))
                    if b.follows():
                        dve.wait_ge(yT_mm.sem, yT_mm.at(b, back=1))
                    for t in range(TT):
                        dve.tensor_scalar(mlp_y[:, t, :], halves(7)[:, t, :], q_back[:, t:t + 1], None, ALU.mult)\
                            .then_inc(y_dve.sem, 1)

                def residual_3(b):
                    dve.wait_ge(yT_mm.sem, yT_mm.at(b))
                    dve.wait_ge(x2_cp.sem, x2_cp.at(b))
                    if b.follows():
                        dve.wait_ge(n4_dve.sem, n4_dve.at(b, 2, back=1))
                    dve.tensor_tensor(x3[:], halves(6), x2[:], ALU.add).then_inc(x3_dve.sem, 1)

                def relu(b):
                    dve.wait_ge(ad_mm.sem, ad_mm.at(b))
                    if b.follows():
                        dve.wait_ge(au_mm.sem, au_mm.at(b, back=1))
                    dve.tensor_scalar(adapt_h[:], bank[7][:, 0:T], bd_c[:], 0.0, ALU.add, ALU.max).then_inc(ad_h.sem, 1)

                def residual_4(b):
                    dve.wait_ge(au_mm.sem, au_mm.at(b))
                    for c in range(DC):
                        dve.scalar_tensor_tensor(x3[:, c, :], halves(6)[:, c, :], bu_c[:, c:c + 1], x3[:, c, :], ALU.add, ALU.add)\
                            .then_inc(x4_dve.sem, 1)

                def centre(b):
                    dve.wait_ge(n4_pe.sem, n4_pe.at(b, 1))
                    if b.follows():
                        dve.wait_ge(out_dma.sem, out_dma.at(b, back=1))
                    m = bank[7][:, 0:T]
                    for c in range(DC):
                        dve.tensor_tensor(xc[:, c, :], x3[:, c, :], m, ALU.subtract).then_inc(n4_dve.sem, 1)

                def layer_norm(b):
                    dve.wait_ge(n4_act.sem, n4_act.at(b))
                    newton(b, y4, 6, EPS_LN, n4_dve, 2)

                def run(a, f, g, nxt):
                    if starts(f):
                        dve.wait_ge(consts.sem, 6)
                        dve.wait_ge(ternary.sem, TERNARY)
                    for c in range(FC):
                        if f and c < FC - 1:
                            gated(f, c)
                        if a:
                            row_max(a, 2 * c)
                        if f and c == FC - 1:
                            gated(f, c)
                        if a:
                            row_max(a, 2 * c + 1)
                        if g and 1 <= c <= 4:
                            quantise[c - 1](g, 1)
                        if g and c == 2:
                            q_turned(g, 0)
                    if g:
                        q_turned(g, 1)
                    if f:
                        residual_2(f)
                    if g:
                        scaled_y(g)
                    if nxt:
                        norm_a(nxt)
                    if g:
                        residual_3(g)
                    if f:
                        norm_g(f)
                    if g:
                        relu(g)
                    if a:
                        normalise(a, 0)
                    if f:
                        low_g(f)
                    if g:
                        residual_4(g)
                    if a:
                        normalised(a, 0)
                        normalise(a, 1)
                        normalised(a, 1)
                    if g:
                        centre(g)
                    if nxt:
                        low_qk(nxt)
                    if a:
                        residual_1(a)
                    if g:
                        layer_norm(g)
                    if a:
                        norm_f(a)
                    for n in range(8):
                        if f:
                            gated_u(f, n)
                            if n >= UC:
                                quantise[n - UC](f, 0)
                        if a and n == 0:
                            scaled_f(a)
                        if a and n == 2:
                            low_f(a)

                dve.memset(cond_t[:], 0.0).then_inc(blank.sem, 1)
                dve.memset(mean_w[:], 1.0 / D).then_inc(consts.sem, 1)
                dve.memset(ones[:], 1.0).then_inc(consts.sem, 1)
                dve.memset(eps_rms, EPS_RMS).then_inc(consts.sem, 1)
                dve.memset(eps_ln, EPS_LN).then_inc(consts.sem, 1)
                dve.memset(q_stack[:].bitcast(F32), 0.0).then_inc(init_dve.sem, 1)
                dve.memset(zero_row, 0.0).then_inc(init_dve.sem, 1)
                dve.memset(one_row, 1.0).then_inc(init_dve.sem, 1)
                dve.memset(v_aug[:], 1.0).then_inc(init_dve.sem, 1)
                dve.wait_ge(consts.sem, 4)
                dve.wait_ge(vec_in.sem, 64)
                dve.wait_ge(cond_mm.sem, 1)
                src = bank[5][:, 0:16 * NB].rearrange("p (m c b) -> p m c b", m=8, c=DC)
                dve.wait_ge(tanh_act.sem, DC)
                dve.tensor_scalar(par[:, A_GAMMA], src[:, 0], -0.5, None, ALU.mult).then_inc(table.sem, 1)
                dve.tensor_copy(par[:, A_BETA], src[:, 1]).then_inc(table.sem, 1)
                dve.tensor_scalar(par[:, NEG_ALPHA], src[:, 2], -1.0, None, ALU.mult).then_inc(table.sem, 1)
                dve.tensor_scalar(par[:, F_GAMMA], src[:, 3], -0.5, None, ALU.mult).then_inc(table.sem, 1)
                dve.tensor_copy(par[:, F_BETA], src[:, 4]).then_inc(table.sem, 1)
                dve.tensor_scalar(par[:, L1_SCALE], src[:, 6], 1.0, -0.5, ALU.add, ALU.mult).then_inc(table.sem, 1)
                dve.tensor_copy(par[:, F_ALPHA], src[:, 5]).then_inc(table.sem, 1)
                for c in range(DC):
                    dve.tensor_scalar(tanh_t[:, c, :], tanh_t[:, c, :], ln_b_c[:, c:c + 1], ln_w_c[:, c:c + 1],
                                      ALU.add, ALU.mult).then_inc(table.sem, 1)
                dve.wait_ge(table.sem, 7 + DC)
                for c in range(DC):
                    dve.tensor_scalar(par[:, ALPHA_B, c, :], par[:, F_ALPHA, c, :], out_b_c[:, c:c + 1], None,
                                      ALU.mult).then_inc(table.sem, 1)
                    dve.tensor_scalar(par[:, OFFSET, c, :], tanh_t[:, c, :], ln_b_c[:, c:c + 1], None, ALU.add)\
                        .then_inc(table.sem, 1)
                dve.wait_ge(table.sem, 7 + 3 * DC)
                dve.tensor_copy(par_t[:].rearrange("p b k c -> p k c b"), par[:]).then_inc(table.sem, 1)
                dve.tensor_copy(par_a1[:], par[:, A_GAMMA:A_BETA + 1, :, 0]).then_inc(par_ready.sem, 1)
                dve.wait_ge(par_ready.sem, 1)
                norm_a(Batch(0))
                low_qk(Batch(0))
                dve.wait_ge(small_in.sem, 16 * 6)
                dve.wait_ge(table.sem, TABLE - 1)
                dve.scalar_tensor_tensor(adapt_base[:], adapt_bias[:], 0.1, adapt_base[:], ALU.mult, ALU.add)\
                    .then_inc(table.sem, 1)
                dve.tensor_copy(ident_bf[:], ident[:]).then_inc(consts.sem, 1)
                dve.scalar_tensor_tensor(neg_w2[:], ln_w_c[:], -0.5, ln_w_c[:], ALU.mult, ALU.mult).then_inc(consts.sem, 1)
                dve.wait_ge(down_in.sem, 16)
                dve.tensor_reduce(w_abs, w_down, AX_X, ALU.add, apply_absolute_value=True).then_inc(ternary.sem, 1)
                dve.wait_ge(abs_mm.sem, 1)
                dve.tensor_scalar(w_mean, bank[5][:, 0:1], 1.0 / (F * D), 1e-5, ALU.mult, ALU.max).then_inc(ternary.sem, 1)
                dve.wait_ge(ternary.sem, 2)
                dve.reciprocal(w_rec, w_mean).then_inc(ternary.sem, 1)
                dve.wait_ge(ternary.sem, 3)
                dve.reciprocal(down_scale[:], w_rec).then_inc(ternary.sem, 1)
                w_part = adapt_bias
                dve.wait_ge(table.sem, TABLE)
                down_all = down[:].rearrange("p c n -> p (c n)")
                for n in range(4):
                    part = slice(512 * n, 512 * (n + 1))
                    dve.wait_ge(ternary.sem, 4 + 3 * n)
                    dve.tensor_scalar(w_part[:], w_down[:, part], w_rec, MAGIC, ALU.mult, ALU.add).then_inc(ternary.sem, 1)
                    dve.wait_ge(ternary.sem, 5 + 3 * n)
                    dve.tensor_scalar(w_part[:], w_part[:], MAGIC, 1.0, ALU.subtract, ALU.min).then_inc(ternary.sem, 1)
                    dve.wait_ge(ternary.sem, 6 + 3 * n)
                    dve.tensor_scalar(down_all[:, part], w_part[:], -1.0, None, ALU.max).then_inc(ternary.sem, 1)
                whole(dve, run)


_OUT = (NB, D, T)


def kernel(**inputs):
    import numpy as np
    import concourse.bacc as bacc
    from concourse.bass_utils import run_bass_kernel_spmd

    v = {k: np.asarray(a) for k, a in inputs.items()}
    t = lambda name: v[name].T
    wdd = v["L2_cond_Wdd"].reshape(BN, D, C).transpose(2, 1, 0).reshape(C, D * BN)
    wdu = v["L2_cond_Wdu"].reshape(D, BN, C).transpose(2, 1, 0).reshape(C, D * BN)

    def chunked(a):
        return a.reshape(DC, P, BN).transpose(1, 0, 2).reshape(P, DC * BN)

    arrays = {
        "xT": v["x"].transpose(0, 2, 1),
        "condT": t("cond_256"),
        "w_cond": np.concatenate([t(n) for n in (
            "L0_cond_attn_gamma_w", "L0_cond_attn_beta_w", "L0_cond_attn_alpha_w", "L0_cond_ffn_gamma_w",
            "L0_cond_ffn_beta_w", "L0_cond_ffn_alpha_w", "L1_cond_norm_w", "L3_cond_lin_w")], axis=1),
        "w_qkvT": np.concatenate([t("L0_cond_W_q"), t("L0_cond_W_k"), t("L0_cond_W_v")], axis=1),
        "w_oT": t("L0_cond_W_o").reshape(DC, 2, 4, DH, D).transpose(0, 2, 1, 3, 4).reshape(D, D),
        "head_rows": np.stack([(np.arange(P) // DH + 1) % 2, np.arange(P) // DH % 2], axis=1).astype(np.float32),
        "w_ghT": np.concatenate([t("L0_cond_gate_w"), t("L0_cond_hidden_w")], axis=1),
        "w_outT": t("L0_cond_out_w"),
        "out_b": v["L0_cond_out_b"].reshape(DC, P).T,
        "w_upT": t("L1_cond_up_w"),
        "w_downT": t("L1_cond_down_w"),
        "w_hyper": np.concatenate([wdd, wdu], axis=0),
        "adapt_w": np.concatenate([chunked(t("L2_cond_Wd")), t("L2_cond_Wu")], axis=1),
        "adapt_b": np.concatenate([chunked(v["L2_cond_bdd"].reshape(BN, D).T), v["L2_cond_bdu"].reshape(D, BN).T], axis=1),
        "bd": v["L2_cond_bd"].reshape(BN, 1),
        "bu": v["L2_cond_bu"].reshape(DC, P).T,
        "ln_w": v["L3_cond_weight"].reshape(DC, P).T,
        "ln_b": v["L3_cond_bias"].reshape(DC, P).T,
        "lin_b": v["L3_cond_lin_b"].reshape(DC, P).T,
        "ident_in": np.eye(P, dtype=np.float32),
    }
    arrays = {k: np.ascontiguousarray(a) for k, a in arrays.items()}
    nc = bacc.Bacc("TRN2", target_bir_lowering=False, num_devices=1)
    args = {k: nc.dram_tensor(k, a.shape, mybir.dt.from_np(a.dtype), kind="ExternalInput").ap() for k, a in arrays.items()}
    out = nc.dram_tensor("out", _OUT, F32, kind="ExternalOutput").ap()
    build(nc, **args, out=out)
    r = run_bass_kernel_spmd(nc, [arrays], core_ids=[0])
    return np.asarray(r.results[0]["out"]).transpose(0, 2, 1)
```
